# Optimizing a Trainium2 kernel written in Bass

```python
import numpy as np
import jax
import jax.numpy as jnp

def _softmax(x, axis=-1):
    return jax.nn.softmax(x, axis=axis)

def _gelu(x):
    return jax.nn.gelu(x, approximate=True)

def _silu(x):
    return jax.nn.silu(x)

def _sigmoid(x):
    return jax.nn.sigmoid(x)

def _layernorm(x, axis=-1, eps=1e-05):
    m = jnp.mean(x, axis=axis, keepdims=True)
    v = jnp.var(x, axis=axis, keepdims=True)
    return (x - m) / jnp.sqrt(v + eps)

def _scatter_add(tgt, idx, src, axis=0):
    return tgt.at[idx].add(src)

def _segment_sum(src, seg, n):
    return jax.ops.segment_sum(src, seg, n)
kernel_name = 'mk_gnn_resnorm_d1_gnn_r64_62be96'

def setup_inputs(seed: int=0):
    np.random.seed(seed)
    _w = jnp.asarray

    def _rec_inputs():
        import jax
        import jax.numpy as jnp
        _gk = jax.random.key(seed)
        x = -0.0002117 + 1 * jax.random.normal(jax.random.fold_in(_gk, 1), (100000, 256), jnp.float32)
        _s = jax.random.randint(jax.random.fold_in(_gk, 2), (12500,), 0, 100000, jnp.int32)
        _d = jax.random.randint(jax.random.fold_in(_gk, 3), (12500,), 0, 100000, jnp.int32)
        _loop = jnp.arange(100000, dtype=jnp.int32)
        src = jnp.concatenate([_s, _d, _loop])
        dst = jnp.concatenate([_d, _s, _loop])
        _o = jnp.argsort(dst, stable=True)
        src = src[_o]
        dst = dst[_o]
        return (x, src, dst)
    x, src, dst = _rec_inputs()

    def _L0_gnn_setup():
        import jax, jax.numpy as jnp
        import numpy as np
        N, D_DIM, K, R = (100000, 256, 4, 16)
        E_RAND = 25000
        ETA, LAM, C = (0.5, 0.1, 0.5)
        key = jax.random.key(seed)
        k1, k2, k3, k4 = jax.random.split(key, 4)
        Z = jax.random.normal(k1, (N, D_DIM), jnp.float32)
        U = jax.random.normal(k2, (K, D_DIM, R), jnp.float32) / np.float32(np.sqrt(D_DIM))
        Dmat = jax.random.normal(k3, (D_DIM, D_DIM), jnp.float32) / np.float32(np.sqrt(D_DIM))
        head_w = jnp.ones((K,), jnp.float32) / K
        rnd = jax.random.randint(k4, (2, E_RAND), 0, N)
        loops = jnp.stack([jnp.arange(N), jnp.arange(N)])
        edge_index = jnp.concatenate([rnd, loops], axis=1)
        return {'Z': Z, 'U': U, 'Dmat': Dmat, 'head_w': head_w, 'edge_index': edge_index}
    _L0_gnn_all = _L0_gnn_setup()
    _L0_gnn_in = {k: v for k, v in _L0_gnn_all.items() if k in ('U', 'Dmat', 'head_w')}
    del _L0_gnn_all
    return {'x': x, 'src': src, 'dst': dst, 'L0_gnn_U': _L0_gnn_in['U'], 'L0_gnn_Dmat': _L0_gnn_in['Dmat'], 'L0_gnn_head_w': _L0_gnn_in['head_w']}

def reference(x, src, dst, L0_gnn_U, L0_gnn_Dmat, L0_gnn_head_w):
    import jax
    import jax.numpy as jnp

    def _L0_gnn_ref(Z, U, Dmat, head_w, edge_index):
        import jax, jax.numpy as jnp
        import numpy as np
        N, D_DIM, K, R = (100000, 256, 4, 16)
        E_RAND = 25000
        ETA, LAM, C = (0.5, 0.1, 0.5)
        src, dst = (edge_index[0], edge_index[1])
        scale = np.float32(np.sqrt(R))
        ZU = jnp.einsum('nd,kdr->knr', Z, U)
        zs = ZU[:, src, :]
        zd = ZU[:, dst, :]
        logits = (zs * zd).sum(-1) / scale
        seg_max = jax.vmap(lambda l: jax.ops.segment_max(l, dst, num_segments=N))(logits)
        exp_l = jnp.exp(logits - seg_max[:, dst])
        seg_sum = jax.vmap(lambda e: jax.ops.segment_sum(e, dst, num_segments=N))(exp_l)
        alpha = exp_l / (seg_sum[:, dst] + 1e-16)
        weighted = alpha[..., None] * zs
        agg = jax.vmap(lambda w_: jax.ops.segment_sum(w_, dst, num_segments=N))(weighted)
        w = jax.nn.softmax(head_w)
        ssa = jnp.einsum('k,knr,kdr->nd', w, agg, U)
        Z_half = (1.0 - C) * Z + C * ssa
        DZ = Z_half @ Dmat.T
        residual = Z_half - DZ @ Dmat
        grad_step = Z_half + ETA * (residual @ Dmat)
        return jax.nn.relu(grad_step - ETA * LAM)
    edge_index = jnp.stack([src, dst])
    x = _layernorm(x + _L0_gnn_ref(x, L0_gnn_U, L0_gnn_Dmat, L0_gnn_head_w, edge_index), axis=-1)
    return x

_drawn_inputs = setup_inputs


def setup_inputs(seed=0):
    import zlib

    import numpy as np

    out = dict(_drawn_inputs(seed))
    spreads = {'L0_gnn_head_w': (0.25, 0.2)}
    factors = {}
    for name, (base, spread) in spreads.items():
        noise = np.random.default_rng([zlib.crc32(name.encode()), seed]).standard_normal(out[name].shape)
        drawn = base * np.exp(spread * noise) if base else spread * noise
        out[name] = jnp.asarray(drawn.astype(out[name].dtype))
    for name, factor in factors.items():
        out[name] = (out[name] * factor).astype(out[name].dtype)
    return out
```

```python
import concourse.bass as bass
from concourse import mybir
from contextlib import ExitStack

N, D, K, R, E = 100000, 256, 4, 16, 125000
F = K * R
P = 128
HALVES = D // P
ETA, LAM, C = 0.5, 0.1, 0.5
EPS_SUM, EPS_LN = 1e-16, 1e-5
BIG = 1.0e38

BN = 1024
BT = BN // P
HB = BN // 2
HT = BT // 2
NBLOCKS = -(-N // BN)
LAST_BASE = N - BN
BPAIRS = NBLOCKS // 2

ET = 125
TG = 25
GE = ET * TG
GROUPS = E // GE
GPAIRS = GROUPS // 2
TILES = GROUPS * TG
WIN = P
CT = 5
CHUNKS = TG // CT
KJ = K * TG
IQ = 8
SPR = TG + 1


def build(nc, x, src, dst, U, Dmat, head_w, out):
    f32, i32 = mybir.dt.float32, mybir.dt.int32
    ALU, ACT, AX = mybir.AluOpType, mybir.ActivationFunctionType, mybir.AxisListType
    ctx = ExitStack()
    with ctx:
        def sb(name, shape, dt=f32):
            return ctx.enter_context(nc.sbuf_tensor(name, shape, dt))

        def sem(name):
            return ctx.enter_context(nc.semaphore(name))

        def sem2(name):
            return [sem(f"{name}{p}") for p in range(2)]

        ps = [ctx.enter_context(nc.psum_tensor(f"bank{b}", [P, 512], f32)) for b in range(8)]

        z_dram = nc.dram_tensor("z_dram", [N + WIN, F], f32).ap()
        agg_dram = nc.dram_tensor("agg_dram", [2 * F, N + GE], f32).ap()
        dst_pad = nc.dram_tensor("dst_pad", [1, E + 2], i32).ap()

        ident = sb("ident", [P, P])
        iota_i = sb("iota_i", [P, P + 1], i32)
        iota_row = sb("iota_row", [P, P])
        iota_col = sb("iota_col", [P, 1])
        ones = sb("ones", [1, P])
        minus1 = sb("minus1", [1, 1], i32)
        U_sb = sb("U_sb", [P, HALVES, F])
        Uw = sb("Uw", [P, HALVES, 2, F])
        D_sb = sb("D_sb", [P, HALVES, D])
        DtD = sb("DtD", [P, HALVES, D])
        Mh = sb("Mh", [P, HALVES, D])
        G2 = sb("G2", [P, D])
        hw = sb("hw", [P, K])
        hwm = sb("hwm", [P, 1])
        hws = sb("hws", [P, 1])
        src_col = sb("src_col", [ET, TILES], i32)
        dst_col = sb("dst_col", [ET, TILES])
        first_all = sb("first_all", [P, TILES])
        node_col = sb("node_col", [P, TILES])
        dst_rel = sb("dst_rel", [ET, TILES])
        first_i = sb("first_i", [1, TILES], i32)
        off_i = sb("off_i", [1, TILES], i32)
        gap_i = sb("gap_i", [1, GROUPS], i32)
        xs = [sb(f"xs{p}", [P, 2, HT, D]) for p in range(2)]
        xT = [sb(f"xT{p}", [P, 2, HALVES, P]) for p in range(2)]
        zo = [sb(f"zo{p}", [P, 2, HT, F]) for p in range(2)]
        idx_g = [sb(f"idx_g{p}", [ET, TG], i32) for p in range(2)]
        zs = [sb(f"zs{p}", [ET, TG, F]) for p in range(2)]
        zw = [sb(f"zw{p}", [WIN, TG, F]) for p in range(2)]
        dst_b = [sb(f"dst_b{p}", [P, TG, ET], i32) for p in range(2)]
        rows_i = [sb(f"rows_i{p}", [KJ, ET + 2], i32) for p in range(2)]
        nodes_g = sb("nodes_g", [P, TG])
        rel_g = sb("rel_g", [ET, TG])
        spread = [sb(f"spread{p}", [WIN, CT, ET]) for p in range(2)]
        onehot = sb("onehot", [P, TG, WIN])
        prod = sb("prod", [ET, CT, K, R])
        logit = sb("logit", [ET, K, TG])
        rows = sb("rows", [KJ, ET + 2])
        pen = sb("pen", [KJ, ET + 1])
        pen_first = sb("pen_first", [KJ, ET])
        pen_last = sb("pen_last", [KJ, ET])
        fmax = sb("fmax", [KJ, ET])
        rmax = sb("rmax", [KJ, ET])
        m1 = sb("m1", [KJ, ET])
        m2 = sb("m2", [KJ, ET])
        shifted = sb("shifted", [KJ, ET])
        edge4 = sb("edge4", [1, 4, KJ])
        differ = sb("differ", [1, 2, KJ])
        fpen = sb("fpen", [1, K, SPR])
        bpen = sb("bpen", [1, K, SPR])
        fval = sb("fval", [1, K, SPR])
        bval = sb("bval", [1, K, SPR])
        run = sb("run", [1, K, SPR])
        back = sb("back", [1, K, SPR])
        beside = sb("beside", [1, 2, KJ])
        rrow = sb("rrow", [1, 2, K, R])
        rrow2 = sb("rrow2", [1, 2, K, R])
        rscale = sb("rscale", [P, 1])
        W = sb("W", [P, TG, 2, F])
        agg = [sb(f"agg{p}", [P, GE + WIN]) for p in range(2)]
        raw_i = dst_b[0][:ET, :, :].rearrange("p t e -> p (t e)")[:, 0:2 * ET * IQ].rearrange("p (s c) -> p s c", s=2)
        raw_f = W[:ET, :, :, :].rearrange("p t a f -> p (t a f)")[:, 0:2 * ET * IQ].rearrange("p (s c) -> p s c", s=2)
        nd = [agg[p][:, 0:2 * HB].rearrange("q (a n) -> q a n", a=2) for p in range(2)]
        aggn = [agg[p][:, 2 * HB:3 * HB].rearrange("q (t n) -> q t n", t=HT) for p in range(2)]
        hb = [onehot[:, :, :].rearrange("p t n -> p (t n)")[:, 0:BT * D].rearrange("p (h t d) -> p h t d", h=2, t=HT),
              W[:, :, :, :].rearrange("p t a f -> p (t a f)")[:, 0:BT * D].rearrange("p (h t d) -> p h t d", h=2, t=HT)]
        stats = sb("stats", [P, BT, 6])
        mv = [sb(f"mv{p}", [P, BT, 2]) for p in range(2)]
        std = [sb(f"std{p}", [P, BT]) for p in range(2)]
        rstd = [sb(f"rstd{p}", [P, BT]) for p in range(2)]
        nmr = [sb(f"nmr{p}", [P, BT]) for p in range(2)]

        const_step = sem("const_step")
        w_in = sem("w_in")
        pad_out = sem("pad_out")
        idx_float = sem("idx_float")
        idx_ps = sem("idx_ps")
        idx_sb = sem("idx_sb")
        prep_pe = sem("prep_pe")
        prep_dve = sem("prep_dve")
        prep_act = sem("prep_act")
        gate = sem("gate")
        x_in = sem2("x_in")
        xt_ps = sem2("xt_ps")
        xt_sb = [sem(f"xt_sb{m}") for m in range(2)]
        xt_used = [sem(f"xt_used{m}") for m in range(2)]
        z_sb = sem2("z_sb")
        z_out = sem2("z_out")
        idx_ready = sem2("idx_ready")
        gathered = sem2("gathered")
        zw_in = sem2("zw_in")
        rows_in = sem2("rows_in")
        cols_g = sem("cols_g")
        spread_done = sem2("spread_done")
        zd_ps = sem2("zd_ps")
        prod_done = sem2("prod_done")
        logit_done = sem2("logit_done")
        oh_done = sem("oh_done")
        flag_step = sem("flag_step")
        flag_ps = sem("flag_ps")
        lrow_ps = sem("lrow_ps")
        scan_step = sem("scan_step")
        ab_ps = sem("ab_ps")
        chain_step = sem("chain_step")
        li_ps = sem("li_ps")
        r_exp = sem("r_exp")
        r_ps = sem("r_ps")
        shifted_ps = sem("shifted_ps")
        p_done = sem("p_done")
        w_done = sem2("w_done")
        agg_ps = sem("agg_ps")
        agg_step = sem("agg_step")
        flushed = sem2("flushed")
        x2_in = sem2("x2_in")
        nd_in = sem2("nd_in")
        nd_step = sem2("nd_step")
        xt2_ps = sem2("xt2_ps")
        xt2_sb = [sem(f"xt2_sb{m}") for m in range(2)]
        g_ps = sem2("g_ps")
        h_done = sem2("h_done")
        stat_step = sem2("stat_step")
        std_done = sem2("std_done")
        norm_step = sem2("norm_step")
        normed = sem2("normed")
        out_done = sem2("out_done")

        CONSTS = 13
        W_IN = 16 * 9
        PREP_IDX = 9
        PREP = 21
        FLAG, SCAN, CHAIN, AGG = 9, 5, 9, 2 + 2 * TG

        def block_base(b):
            return LAST_BASE if isinstance(b, int) and b == NBLOCKS - 1 else b * BN

        def block_rows(t, base):
            return t[bass.ds(base, BN), :].rearrange("(h p t) d -> p h (t d)", h=2, t=HT)

        def block_pairs(eng, body):
            with eng.Fori(0, BPAIRS - 1) as i:
                for par in range(2):
                    body(i, par, i * 2 + par)
            for par in range(2):
                body(BPAIRS - 1, par, 2 * (BPAIRS - 1) + par)

        def group_pairs(eng, body):
            with eng.Fori(0, GPAIRS) as i:
                for par in range(2):
                    body(i, par, i * 2 + par)

        def passed(eng):
            eng.sem_inc(gate, 1)

        block = ctx.enter_context(nc.Block())

        @block.sync
        def _(sp):
            for h in range(HALVES):
                sp.dma_start(U_sb[:, h, :].rearrange("p (k r) -> p k r", k=K),
                             U[:, h * P:(h + 1) * P, :].rearrange("k p r -> p k r")).then_inc(w_in, 16)
                sp.dma_start(D_sb[:, h, :], Dmat[h * P:(h + 1) * P, :]).then_inc(w_in, 16)
            sp.dma_start(hw[:, :], head_w.rearrange("(a k) -> a k", a=1).to_broadcast([P, K])).then_inc(w_in, 16)
            sp.dma_start(raw_i[:, 0, :], src.rearrange("(q c) -> q c", q=ET)).then_inc(w_in, 16)
            sp.dma_start(raw_i[:, 1, :], dst.rearrange("(q c) -> q c", q=ET)).then_inc(w_in, 16)
            sp.dma_start(dst_pad[0:1, 1:E + 1].rearrange("a (q c) -> (a q) c", q=ET),
                         dst.rearrange("(q c) -> q c", q=ET)).then_inc(pad_out, 16)
            sp.wait_ge(const_step, 3)
            sp.dma_start(dst_pad[0:1, 0:1], minus1[:, :]).then_inc(w_in, 16)
            sp.dma_start(dst_pad[0:1, E + 1:E + 2], minus1[:, :]).then_inc(w_in, 16)
            sp.wait_ge(const_step, 4)
            sp.dma_start(z_dram[N:N + WIN, :], agg[0][:, 0:F]).then_inc(pad_out, 16)

            def load_x(i, par, b):
                sp.wait_ge(xt_ps[par], 4 * i)
                sp.dma_start(xs[par][:, :, :, :].rearrange("p h t d -> p h (t d)"),
                             block_rows(x, block_base(b))).then_inc(x_in[par], 16)
            block_pairs(sp, load_x)

            sp.wait_ge(prep_dve, PREP_IDX)
            sp.wait_ge(pad_out, 32)
            sp.wait_ge(w_in, W_IN)
            for par in range(2):
                sp.wait_ge(z_out[par], 16 * BPAIRS)

            def load_group(i, par, g):
                sp.wait_ge(spread_done[par], CHUNKS * i)
                sp.dma_start(dst_b[par][:, :, :].rearrange("p t e -> p (t e)"),
                             dst_pad[0:1, bass.ds(g * GE + 1, GE)].to_broadcast([P, GE])).then_inc(rows_in[par], 16)
                v = dst_pad[0:1, bass.ds(g * GE, GE)].rearrange("a (t e) -> (a t) e", t=TG)
                v = bass.AP(v.tensor, v.offset, [[ET, TG], [1, ET + 2]], runtime_checks=v.runtime_checks)
                for k in range(K):
                    sp.dma_start(rows_i[par][k * TG:(k + 1) * TG, :], v).then_inc(rows_in[par], 16)
                sp.wait_ge(zd_ps[par], CHUNKS * i)
                passed(sp)
                for t in range(TG):
                    n0 = sp.value_load(first_i[0:1, bass.ds(g * TG + t, 1)], min_val=0, max_val=N - 1)
                    sp.dma_start(zw[par][:, t, :], z_dram[bass.ds(n0, WIN), :]).then_inc(zw_in[par], 16)

            def flush(i, par, g):
                sp.wait_ge(agg_step, (g + 1) * AGG)
                passed(sp)
                sp.wait_ge(flushed[1 - par], 16 * (i + par))
                passed(sp)
                n0 = sp.value_load(first_i[0:1, bass.ds(g * TG, 1)], min_val=0, max_val=N - 1)
                sp.dma_start(agg_dram[:, bass.ds(n0, GE)], agg[par][:, 0:GE]).then_inc(flushed[par], 16)

            load_group(0, 0, 0)
            with sp.Fori(0, GPAIRS - 1) as i:
                load_group(i, 1, i * 2 + 1)
                flush(i, 0, i * 2)
                load_group(i + 1, 0, i * 2 + 2)
                flush(i, 1, i * 2 + 1)
            load_group(GPAIRS - 1, 1, GROUPS - 1)
            flush(GPAIRS - 1, 0, GROUPS - 2)
            flush(GPAIRS - 1, 1, GROUPS - 1)

            for par in range(2):
                sp.wait_ge(flushed[par], 16 * GPAIRS)

            def load_c(i, par, b):
                base = block_base(b)
                sp.wait_ge(h_done[par], 4 * i)
                sp.dma_start(xs[par][:, :, :, :].rearrange("p h t d -> p h (t d)"),
                             block_rows(x, base)).then_inc(x2_in[par], 16)
                sp.wait_ge(nd_step[par], 3 * i)
                passed(sp)
                for h in range(2):
                    sp.dma_start(nd[par][h * F:(h + 1) * F, :, :],
                                 agg_dram[:, bass.ds(base + h * HB, HB)].rearrange("(a f) n -> f a n", a=2)
                                 ).then_inc(nd_in[par], 16)
            block_pairs(sp, load_c)
            for par in range(2):
                sp.wait_ge(out_done[par], 16 * BPAIRS)

        @block.gpsimd
        def _(pool):
            pool.memset(ident[:, :], 0.0).then_inc(const_step, 1)
            pool.memset(ones[:, :], 1.0).then_inc(const_step, 1)
            pool.memset(minus1[:, :], -1).then_inc(const_step, 1)
            pool.memset(agg[0][:, :], 0.0).then_inc(const_step, 1)
            pool.memset(agg[1][:, :], 0.0).then_inc(const_step, 1)
            pool.iota(iota_i[:, 0:P], [[1, P]], base=0, channel_multiplier=0).then_inc(const_step, 1)
            pool.iota(iota_i[:, P:P + 1], [[0, 1]], base=0, channel_multiplier=1).then_inc(const_step, 1)
            pool.wait_ge(const_step, 7)
            pool.affine_select(out=ident[:, :], in_=ident[:, :], compare_op=ALU.not_equal, fill=1.0,
                               base=0, pattern=[[-1, P]], channel_multiplier=1).then_inc(const_step, 1)
            pool.memset(fpen[:, :, 0:1], -BIG).then_inc(const_step, 1)
            pool.memset(bpen[:, :, TG:SPR], -BIG).then_inc(const_step, 1)
            pool.memset(bval[:, :, TG:SPR], -BIG).then_inc(const_step, 1)
            pool.memset(run[:, :, :], -BIG).then_inc(const_step, 1)
            pool.memset(gap_i[:, 0:1], 0).then_inc(const_step, 1)

            def store_z(i, par, b):
                pool.wait_ge(z_sb[par], i + 1)
                if isinstance(b, int) and b == NBLOCKS - 1:
                    pool.wait_ge(z_out[0], 16 * BPAIRS)
                pool.dma_start(z_dram[bass.ds(block_base(b), BN), :].rearrange("(h p t) f -> p h (t f)", h=2, t=HT),
                               zo[par][:, :, :, :].rearrange("p h t f -> p h (t f)")).then_inc(z_out[par], 16)
            block_pairs(pool, store_z)

            pool.wait_ge(prep_dve, PREP_IDX)
            for par in range(2):
                pool.wait_ge(z_out[par], 16 * BPAIRS)

            def gather(i, par, g):
                pool.wait_ge(gathered[par], i * TG * 16)
                pool.tensor_copy(idx_g[par][:, :], src_col[:, bass.ds(g * TG, TG)]).then_inc(idx_ready[par], 1)
                pool.wait_ge(w_done[par], i)
                pool.wait_ge(idx_ready[par], i + 1)
                passed(pool)
                for t in range(TG):
                    pool.indirect_dma_start(
                        out=zs[par][:, t, :], out_offset=None, in_=z_dram[:, :],
                        in_offset=bass.IndirectOffsetOnAxis(ap=idx_g[par][:, t:t + 1], axis=0),
                        ).then_inc(gathered[par], 16)
            group_pairs(pool, gather)

            def normalise(i, par, b):
                pool.wait_ge(norm_step[par], 2 * (i + 1))
                passed(pool)
                for t in range(BT):
                    h, u = t // HT, t % HT
                    pool.tensor_scalar(hb[par][:, h, u, :], hb[par][:, h, u, :],
                                       rstd[par][:, t:t + 1], nmr[par][:, t:t + 1], ALU.mult, ALU.add
                                       ).then_inc(normed[par], 1)
                pool.wait_ge(normed[par], BT * (i + 1))
                if isinstance(b, int) and b == NBLOCKS - 1:
                    pool.wait_ge(out_done[0], 16 * BPAIRS)
                pool.dma_start(block_rows(out, block_base(b)),
                               hb[par][:, :, :, :].rearrange("p h t d -> p h (t d)")).then_inc(out_done[par], 16)
            block_pairs(pool, normalise)

        @block.tensor
        def _(pe):
            pe.wait_ge(const_step, CONSTS)
            n = 0
            for s in range(2):
                for c in range(IQ):
                    pe.wait_ge(idx_float, 2)
                    if n >= 2:
                        pe.wait_ge(idx_sb, n - 1)
                    pe.transpose(ps[n % 2][:ET, 0:ET], raw_f[:, s, c * ET:(c + 1) * ET],
                                 ident[:ET, :ET]).then_inc(idx_ps, 1)
                    n += 1
            pe.wait_ge(idx_sb, 2 * IQ)
            for c in range(2):
                pe.matmul(ps[2 + c][:, 0:TILES // 2], ones[:, :], dst_col[0:1, c * TILES // 2:(c + 1) * TILES // 2],
                          start=True, stop=True).then_inc(prep_pe, 1)
            pe.wait_ge(w_in, W_IN)
            for a in range(HALVES):
                for b in range(HALVES):
                    mm = pe.matmul(ps[4 + a][:, 0:D], D_sb[:, b, a * P:(a + 1) * P], D_sb[:, b, :],
                                   start=b == 0, stop=b == HALVES - 1)
                mm.then_inc(prep_pe, 1)
            pe.wait_ge(prep_act, 3)
            for a in range(HALVES):
                for b in range(HALVES):
                    mm = pe.matmul(ps[6 + a][:, 0:D], DtD[:, b, a * P:(a + 1) * P], D_sb[:, b, :],
                                   start=b == 0, stop=b == HALVES - 1)
                mm.then_inc(prep_pe, 1)
            pe.wait_ge(prep_dve, PREP)
            for h in range(HALVES):
                mm = pe.matmul(ps[4][:, 0:D], Uw[:, h, :, :].rearrange("p a f -> p (a f)"), Mh[:, h, :],
                               start=h == 0, stop=h == HALVES - 1)
            mm.then_inc(prep_pe, 1)

            def transposes(par, m, x_sb, ps_sem):
                for u in range(2):
                    t = 2 * m + u
                    for h in range(HALVES):
                        tr = pe.transpose(ps[m % 2][:, (u * HALVES + h) * P:(u * HALVES + h + 1) * P],
                                          x_sb[:, t // HT, t % HT, h * P:(h + 1) * P], ident[:, :])
                tr.then_inc(ps_sem[par], 1)

            def block_a(i, par, b):
                pe.wait_ge(x_in[par], 16 * (i + 1))

                def zmm(m):
                    n_sb = (2 * i + par) * 2 + m // 2
                    pe.wait_ge(xt_sb[m % 2], n_sb + 1)
                    if m == 0:
                        pe.wait_ge(z_sb[par], i)
                    for u in range(2):
                        t = 2 * m + u
                        for h in range(HALVES):
                            mm = pe.matmul(ps[2 + par][:, t * F:(t + 1) * F], xT[m % 2][:, u, h, :], U_sb[:, h, :],
                                           start=h == 0, stop=h == HALVES - 1)
                    mm.then_inc(xt_used[m % 2], 1)
                for m in range(BT // 2):
                    pe.wait_ge(xt_sb[m % 2], (2 * i + par) * 2 + m // 2)
                    transposes(par, m, xs[par], xt_ps)
                    if m:
                        zmm(m - 1)
                zmm(BT // 2 - 1)
            block_pairs(pe, block_a)

            def group_b(i, par, g):
                pe.wait_ge(flag_step, FLAG * g + 1)
                for n, c in enumerate((0, 1, ET, ET + 1)):
                    tr = pe.transpose(ps[6][0:1, n * KJ:(n + 1) * KJ], rows[:, c:c + 1], ident[:KJ, :KJ])
                tr.then_inc(flag_ps, 1)
                pe.wait_ge(zw_in[par], (i + 1) * TG * 16)
                for c in range(CHUNKS):
                    pe.wait_ge(spread_done[par], i * CHUNKS + c + 1)
                    if c >= 2:
                        pe.wait_ge(prod_done[par], i * CHUNKS + c - 1)
                    else:
                        pe.wait_ge(prod_done[1 - par], (i + par) * CHUNKS)
                    for u in range(CT):
                        mm = pe.matmul(ps[2 + c % 2][:ET, u * F:(u + 1) * F], spread[c % 2][:, u, :],
                                       zw[par][:, c * CT + u, :], start=True, stop=True)
                    mm.then_inc(zd_ps[par], 1)
                pe.wait_ge(logit_done[par], (i + 1) * CHUNKS)
                pe.transpose(ps[4][:KJ, 0:ET], logit[:, :, :].rearrange("p k t -> p (k t)"),
                             ident[:ET, :ET]).then_inc(lrow_ps, 1)
                pe.wait_ge(scan_step, SCAN * g + 2)
                pe.transpose(ps[6][0:1, 0:KJ], rmax[:, 0:1], ident[:KJ, :KJ])
                pe.transpose(ps[6][0:1, KJ:2 * KJ], rmax[:, ET - 1:ET], ident[:KJ, :KJ]).then_inc(ab_ps, 1)
                pe.wait_ge(chain_step, CHAIN * g + 7)
                pe.matmul(ps[7][:KJ, 0:1], beside[:, 0, :], ones[:, 0:1], start=True, stop=True)
                pe.matmul(ps[7][:KJ, 1:2], beside[:, 1, :], ones[:, 0:1], start=True, stop=True).then_inc(li_ps, 1)
                pe.wait_ge(r_exp, g + 1)
                pe.matmul(ps[5][:, KJ:KJ + 1], rrow2[0:1, :, :, :].rearrange("a b k r -> a (b k r)"), ones[:, 0:1],
                          start=True, stop=True).then_inc(r_ps, 1)
                pe.wait_ge(scan_step, SCAN * g + 5)
                pe.transpose(ps[5][:ET, 0:KJ], shifted[:, :], ident[:KJ, :KJ]).then_inc(shifted_ps, 1)
                pe.wait_ge(w_done[par], i + 1)
                pe.wait_ge(oh_done, g + 1)
                for t in range(TG):
                    q = t // 4
                    if t % 4 == 0:
                        pe.wait_ge(agg_step, g * AGG + (2 + 8 * (q - 1) if q >= 2 else 0))
                    pe.matmul(ps[q % 2][:, (t % 4) * P:(t % 4 + 1) * P], W[:ET, t, :, :].rearrange("p a f -> p (a f)"),
                              onehot[:ET, t, :], start=True, stop=True).then_inc(agg_ps, 1)
            group_pairs(pe, group_b)

            def block_c(i, par, b):
                pe.wait_ge(x2_in[par], 16 * (i + 1))

                def gmm(m):
                    n_sb = (2 * i + par) * 2 + m // 2
                    pe.wait_ge(xt2_sb[m % 2], n_sb + 1)
                    if m == 0:
                        pe.wait_ge(nd_step[par], 3 * (i + 1))
                    if m >= 2:
                        pe.wait_ge(h_done[par], 4 * i + m - 1)
                    else:
                        pe.wait_ge(h_done[1 - par], 4 * (i + par))
                    for u in range(2):
                        t = 2 * m + u
                        hf, uu = t // HT, t % HT
                        o = ps[4 + m % 2][:, u * D:(u + 1) * D]
                        for h in range(HALVES):
                            pe.matmul(o, xT[m % 2][:, u, h, :], Mh[:, h, :], start=h == 0, stop=False)
                        mm = pe.matmul(o, aggn[par][hf * F:(hf + 1) * F, uu, :], G2[hf * F:(hf + 1) * F, :],
                                       start=False, stop=True)
                    mm.then_inc(g_ps[par], 1)
                for m in range(BT // 2):
                    pe.wait_ge(xt2_sb[m % 2], (2 * i + par) * 2 + m // 2)
                    transposes(par, m, xs[par], xt2_ps)
                    if m:
                        gmm(m - 1)
                gmm(BT // 2 - 1)
            block_pairs(pe, block_c)

        @block.scalar
        def _(act):
            act.wait_ge(prep_dve, PREP_IDX + 2)
            act.activation(hw[:, :], hw[:, :], ACT.Exp, bias=hwm[:, :], accum_out=hws[:, :]).then_inc(prep_act, 1)
            for a in range(HALVES):
                act.wait_ge(prep_pe, 3 + a)
                act.activation(DtD[:, a, :], ps[4 + a][:, 0:D], ACT.Copy).then_inc(prep_act, 1)
            act.wait_ge(prep_pe, 7)
            act.activation(G2[:, :], ps[4][:, 0:D], ACT.Copy).then_inc(prep_act, 1)

            def block_a(i, par, b):
                for m in range(1, BT // 2, 2):
                    act.wait_ge(xt_ps[par], 4 * i + m + 1)
                    act.wait_ge(xt_used[1], (2 * i + par) * 2 + m // 2)
                    act.activation(xT[1][:, :, :, :].rearrange("p u h n -> p (u h n)"), ps[1][:, :], ACT.Copy
                                   ).then_inc(xt_sb[1], 1)
                if par == 1:
                    act.wait_ge(xt_used[1], (2 * i + par + 1) * 2)
                    act.wait_ge(z_out[1], 16 * i)
                    act.activation(zo[1][:, :, :, :].rearrange("p h t f -> p (h t f)"), ps[3][:, :], ACT.Copy
                                   ).then_inc(z_sb[1], 1)
            block_pairs(act, block_a)

            def group_b(i, par, g):
                act.wait_ge(chain_step, CHAIN * g + 9)
                act.wait_ge(r_ps, g)
                act.activation(rrow2[:, :, :, :].rearrange("a b k r -> a (b k r)"),
                               rrow[:, :, :, :].rearrange("a b k r -> a (b k r)"), ACT.Exp).then_inc(r_exp, 1)
                act.wait_ge(shifted_ps, g + 1)
                act.wait_ge(agg_ps, g * TG)
                act.activation(W[:ET, :, 1, :].rearrange("p t (k r) -> p t k r", k=K),
                               ps[5][:ET, 0:KJ].rearrange("p (k t) -> p t k", k=K).unsqueeze(3).to_broadcast([ET, TG, K, R]),
                               ACT.Exp).then_inc(p_done, 1)
                act.wait_ge(r_ps, g + 1)
                act.wait_ge(agg_step, g * AGG)
                act.activation(rscale[:, :], ps[5][:, KJ:KJ + 1], ACT.Copy).then_inc(agg_step, 1)
                act.wait_ge(agg_step, g * AGG + 1)
                act.wait_ge(flushed[par], 16 * i)
                gap = act.value_load(gap_i[0:1, bass.ds(g, 1)], min_val=0, max_val=GE)
                act.activation(agg[par][:, 0:1], agg[1 - par][:, bass.ds(gap, 1)], ACT.Copy, scale=rscale[:, :]
                               ).then_inc(agg_step, 1)
                for t in range(TG):
                    bank = ps[(t // 4) % 2]
                    off = act.value_load(off_i[0:1, bass.ds(g * TG + t, 1)], min_val=0, max_val=GE - 1)
                    if t % 4 == 0:
                        act.wait_ge(agg_ps, g * TG + min(t + 4, TG))
                    act.wait_ge(agg_step, g * AGG + 2 + 2 * t)
                    col = agg[par][:, bass.ds(off, 1)]
                    act.activation(col, bank[:, (t % 4) * P:(t % 4) * P + 1], ACT.Identity, bias=col
                                   ).then_inc(agg_step, 1)
                    act.activation(agg[par][:, bass.ds(off + 1, WIN - 1)], bank[:, (t % 4) * P + 1:(t % 4 + 1) * P],
                                   ACT.Copy).then_inc(agg_step, 1)
            group_pairs(act, group_b)

            def block_c(i, par, b):
                for m in range(BT // 2):
                    act.wait_ge(xt2_ps[par], 4 * i + m + 1)
                    if m >= 2:
                        act.wait_ge(g_ps[par], 4 * i + m - 1)
                    else:
                        act.wait_ge(g_ps[1 - par], 4 * (i + par))
                    act.activation(xT[m % 2][:, :, :, :].rearrange("p u h n -> p (u h n)"), ps[m % 2][:, :], ACT.Copy
                                   ).then_inc(xt2_sb[m % 2], 1)
                act.wait_ge(stat_step[par], (2 * BT + 1) * (i + 1))
                act.activation(std[par][:, :], std[par][:, :], ACT.Sqrt).then_inc(std_done[par], 1)
            block_pairs(act, block_c)

        @block.vector
        def _(dve):
            dve.wait_ge(const_step, CONSTS)
            dve.tensor_copy(iota_row[:, :], iota_i[:, 0:P]).then_inc(prep_dve, 1)
            dve.tensor_copy(iota_col[:, :], iota_i[:, P:P + 1]).then_inc(prep_dve, 1)
            dve.wait_ge(w_in, W_IN)
            dve.tensor_copy(raw_f[:, 0, :], raw_i[:, 0, :]).then_inc(idx_float, 1)
            dve.tensor_copy(raw_f[:, 1, :], raw_i[:, 1, :]).then_inc(idx_float, 1)
            n = 0
            for col in (src_col, dst_col):
                for c in range(IQ):
                    dve.wait_ge(idx_ps, n + 1)
                    dve.tensor_copy(col[:, :].rearrange("p (q j) -> p j q", j=IQ)[:, c, :], ps[n % 2][:ET, 0:ET]
                                    ).then_inc(idx_sb, 1)
                    n += 1
            for c in range(2):
                half = slice(c * TILES // 2, (c + 1) * TILES // 2)
                dve.wait_ge(prep_pe, 1 + c)
                dve.tensor_copy(first_all[:, half], ps[2 + c][:, 0:TILES // 2]).then_inc(prep_dve, 1)
            dve.wait_ge(prep_dve, 4)
            dve.tensor_scalar(node_col[:, :], first_all[:, :], iota_col[:, :], None, ALU.add).then_inc(prep_dve, 1)
            dve.tensor_tensor(dst_rel[:, :], dst_col[:, :], first_all[:ET, :], ALU.subtract).then_inc(prep_dve, 1)
            dve.tensor_copy(first_i[:, :], first_all[0:1, :]).then_inc(prep_dve, 1)
            by_group = first_all[0:1, :].rearrange("a (g t) -> a g t", t=TG)
            dve.tensor_tensor(off_i[:, :].rearrange("a (g t) -> a g t", t=TG), by_group,
                              by_group[:, :, 0:1].to_broadcast([1, GROUPS, TG]), ALU.subtract).then_inc(prep_dve, 1)
            dve.tensor_tensor(gap_i[:, 1:GROUPS], by_group[:, 1:GROUPS, 0], by_group[:, 0:GROUPS - 1, 0],
                              ALU.subtract).then_inc(prep_dve, 1)

            dve.tensor_reduce(hwm[:, :], hw[:, :], AX.X, ALU.max).then_inc(prep_dve, 1)
            dve.wait_ge(prep_dve, PREP_IDX + 1)
            dve.tensor_scalar(hwm[:, :], hwm[:, :], -1.0, None, ALU.mult).then_inc(prep_dve, 1)
            dve.wait_ge(prep_act, 1)
            dve.reciprocal(hws[:, :], hws[:, :]).then_inc(prep_dve, 1)
            dve.wait_ge(prep_dve, PREP_IDX + 3)
            dve.tensor_scalar(hw[:, :], hw[:, :], hws[:, :], None, ALU.mult).then_inc(prep_dve, 1)
            dve.wait_ge(prep_dve, PREP_IDX + 4)
            for a in range(2):
                dve.tensor_tensor(Uw[:, :, a, :].rearrange("p h (k r) -> p h k r", k=K),
                                  U_sb[:, :, :].rearrange("p h (k r) -> p h k r", k=K),
                                  hw[:, :].unsqueeze(1).unsqueeze(3).to_broadcast([P, HALVES, K, R]), ALU.mult
                                  ).then_inc(prep_dve, 1)
            for a in range(HALVES):
                dve.wait_ge(prep_pe, 5 + a)
                dve.tensor_tensor(Mh[:, a, :], D_sb[:, a, :], ps[6 + a][:, 0:D], ALU.subtract).then_inc(prep_dve, 1)
            dve.wait_ge(prep_dve, PREP_IDX + 8)
            for a in range(HALVES):
                dve.tensor_scalar(Mh[:, a, :], Mh[:, a, :], C * ETA, None, ALU.mult).then_inc(prep_dve, 1)
            dve.wait_ge(prep_dve, PREP_IDX + 10)
            for a in range(HALVES):
                diag = Mh[:, a, a * P:(a + 1) * P]
                dve.scalar_tensor_tensor(diag, ident[:, :], C, diag, ALU.mult, ALU.add).then_inc(prep_dve, 1)

            def block_a(i, par, b):
                for m in range(0, BT // 2, 2):
                    dve.wait_ge(xt_ps[par], 4 * i + m + 1)
                    dve.wait_ge(xt_used[0], (2 * i + par) * 2 + m // 2)
                    dve.tensor_copy(xT[0][:, :, :, :].rearrange("p u h n -> p (u h n)"), ps[0][:, :]
                                    ).then_inc(xt_sb[0], 1)
                if par == 0:
                    dve.wait_ge(xt_used[1], (2 * i + par + 1) * 2)
                    dve.wait_ge(z_out[0], 16 * i)
                    dve.tensor_copy(zo[0][:, :, :, :].rearrange("p h t f -> p (h t f)"), ps[2][:, :]
                                    ).then_inc(z_sb[0], 1)
            block_pairs(dve, block_a)

            def group_b(i, par, g):
                flag, scan, chain = FLAG * g, SCAN * g, CHAIN * g
                dve.wait_ge(spread_done[1 - par], (i + par) * CHUNKS)
                dve.wait_ge(oh_done, g)
                dve.wait_ge(flag_step, flag)
                dve.wait_ge(scan_step, scan)
                dve.wait_ge(chain_step, chain)
                dve.tensor_copy(nodes_g[:, :], node_col[:, bass.ds(g * TG, TG)]).then_inc(cols_g, 1)
                dve.tensor_copy(rel_g[:, :], dst_rel[:, bass.ds(g * TG, TG)]).then_inc(cols_g, 1)
                dve.wait_ge(rows_in[par], 16 * (K + 1) * (i + 1))
                dve.wait_ge(flag_ps, g)
                dve.tensor_copy(rows[:, :], rows_i[par][:, :]).then_inc(flag_step, 1)
                dve.wait_ge(flag_step, flag + 1)
                dve.tensor_tensor(pen[:, :], rows[:, 1:ET + 2], rows[:, 0:ET + 1], ALU.not_equal).then_inc(flag_step, 1)
                dve.tensor_scalar(pen_first[:, :], rows[:, 1:ET + 1], rows[:, 0:1], -BIG, ALU.not_equal, ALU.mult
                                  ).then_inc(flag_step, 1)
                dve.tensor_scalar(pen_last[:, :], rows[:, 1:ET + 1], rows[:, ET + 1:ET + 2], -BIG,
                                  ALU.not_equal, ALU.mult).then_inc(flag_step, 1)
                dve.wait_ge(flag_step, flag + 2)
                dve.tensor_scalar(pen[:, :], pen[:, :], -BIG, None, ALU.mult).then_inc(flag_step, 1)

                def spreads(c):
                    if c == 0:
                        dve.wait_ge(cols_g, 2 * (g + 1))
                    if c >= 2:
                        dve.wait_ge(zd_ps[par], i * CHUNKS + c - 1)
                    else:
                        dve.wait_ge(zd_ps[1 - par], (i + par) * CHUNKS)
                    for u in range(CT):
                        t = c * CT + u
                        last = dve.tensor_scalar(spread[c % 2][:, u, :], dst_b[par][:, t, :], nodes_g[:, t:t + 1],
                                                 None, ALU.is_equal)
                    last.then_inc(spread_done[par], 1)

                def logits(c):
                    dve.wait_ge(zd_ps[par], i * CHUNKS + c + 1)
                    if c == 0:
                        dve.wait_ge(gathered[par], 16 * TG * (i + 1))
                        dve.wait_ge(lrow_ps, g)
                        dve.wait_ge(logit_done[1 - par], (i + par) * CHUNKS)
                    else:
                        dve.wait_ge(logit_done[par], i * CHUNKS + c)
                    dve.scalar_tensor_tensor(prod[:, :, :, :].rearrange("p t k r -> p (t k r)"),
                                             ps[2 + c % 2][:ET, 0:CT * F], float(R) ** -0.5,
                                             zs[par][:, c * CT:(c + 1) * CT, :].rearrange("p t f -> p (t f)"),
                                             ALU.mult, ALU.mult).then_inc(prod_done[par], 1)
                    dve.wait_ge(prod_done[par], i * CHUNKS + c + 1)
                    dve.tensor_reduce(logit[:, :, c * CT:(c + 1) * CT].rearrange("p k t -> p t k"),
                                      prod[:, :, :, :], AX.X, ALU.add).then_inc(logit_done[par], 1)

                def onehots(a, b):
                    if a == 0:
                        dve.wait_ge(agg_ps, g * TG)
                    for t in range(a, b):
                        last = dve.tensor_scalar(onehot[:ET, t, :], iota_row[:ET, :], rel_g[:, t:t + 1], None, ALU.is_equal)
                    if b == TG:
                        last.then_inc(oh_done, 1)

                spreads(0)
                spreads(1)
                for c in range(CHUNKS):
                    logits(c)
                    if c + 2 < CHUNKS:
                        spreads(c + 2)
                dve.wait_ge(flag_ps, g + 1)
                dve.tensor_copy(edge4[:, :, :].rearrange("a n k -> a (n k)"), ps[6][0:1, 0:4 * KJ]).then_inc(flag_step, 1)
                dve.tensor_copy(fval[:, :, 0:1], run[:, :, TG:SPR]).then_inc(chain_step, 1)
                onehots(0, 5)
                dve.wait_ge(flag_step, flag + 6)
                dve.tensor_tensor(differ[:, :, :], edge4[:, 0:2, :], edge4[:, 2:4, :], ALU.not_equal).then_inc(flag_step, 1)
                dve.wait_ge(lrow_ps, g + 1)
                dve.wait_ge(flag_step, flag + 7)
                dve.tensor_tensor_scan(fmax[:, :], pen[:, 0:ET], ps[4][:KJ, 0:ET], -BIG, ALU.add, ALU.max
                                       ).then_inc(scan_step, 1)
                dve.tensor_scalar(fpen[:, :, 1:SPR], differ[:, 0, :].rearrange("a (k t) -> a k t", k=K), -BIG, None,
                                  ALU.mult).then_inc(flag_step, 1)
                dve.tensor_scalar(bpen[:, :, 0:TG], differ[:, 1, :].rearrange("a (k t) -> a k t", k=K), -BIG, None,
                                  ALU.mult).then_inc(flag_step, 1)
                dve.wait_ge(scan_step, scan + 1)
                dve.tensor_tensor_scan(rmax[:, ::-1], pen[:, ET:0:-1], fmax[:, ::-1], -BIG, ALU.add, ALU.max
                                       ).then_inc(scan_step, 1)
                onehots(5, 10)
                dve.wait_ge(ab_ps, g + 1)
                dve.tensor_copy(bval[:, :, 0:TG], ps[6][0:1, 0:KJ].rearrange("a (k t) -> a k t", k=K)).then_inc(chain_step, 1)
                dve.tensor_copy(fval[:, :, 1:SPR], ps[6][0:1, KJ:2 * KJ].rearrange("a (k t) -> a k t", k=K)
                                ).then_inc(chain_step, 1)
                dve.wait_ge(chain_step, chain + 3)
                dve.wait_ge(flag_step, flag + 9)

                def flat(v):
                    return v[:, :, :].rearrange("a k s -> a (k s)")
                dve.tensor_tensor_scan(flat(run), flat(fpen), flat(fval), -BIG, ALU.add, ALU.max).then_inc(chain_step, 1)
                dve.tensor_tensor_scan(flat(back)[:, ::-1], flat(bpen)[:, ::-1], flat(bval)[:, ::-1], -BIG,
                                       ALU.add, ALU.max).then_inc(chain_step, 1)
                dve.wait_ge(chain_step, chain + 5)
                dve.tensor_copy(beside[:, 0, :].rearrange("a (k t) -> a k t", k=K), run[:, :, 0:TG]).then_inc(chain_step, 1)
                dve.tensor_copy(beside[:, 1, :].rearrange("a (k t) -> a k t", k=K), back[:, :, 1:SPR]).then_inc(chain_step, 1)
                dve.wait_ge(r_exp, g)
                dve.tensor_tensor(rrow[:, :, :, :], fval[:, :, 0:1].unsqueeze(1).to_broadcast([1, 2, K, R]),
                                  back[:, :, 0:1].unsqueeze(1).to_broadcast([1, 2, K, R]), ALU.subtract).then_inc(chain_step, 1)
                dve.wait_ge(chain_step, chain + 8)
                dve.tensor_scalar(rrow[:, :, :, :], rrow[:, :, :, :], 0.0, None, ALU.min).then_inc(chain_step, 1)
                onehots(10, 15)
                dve.wait_ge(li_ps, g + 1)
                dve.scalar_tensor_tensor(m1[:, :], pen_first[:, :], ps[7][:KJ, 0:1], rmax[:, :], ALU.add, ALU.max
                                         ).then_inc(scan_step, 1)
                dve.wait_ge(scan_step, scan + 3)
                dve.scalar_tensor_tensor(m2[:, :], pen_last[:, :], ps[7][:KJ, 1:2], m1[:, :], ALU.add, ALU.max
                                         ).then_inc(scan_step, 1)
                dve.wait_ge(scan_step, scan + 4)
                dve.tensor_tensor(shifted[:, :], ps[4][:KJ, 0:ET], m2[:, :], ALU.subtract).then_inc(scan_step, 1)
                onehots(15, TG)
                dve.wait_ge(p_done, g + 1)
                dve.tensor_tensor(W[:ET, :, 0, :], zs[par][:, :, :], W[:ET, :, 1, :], ALU.mult).then_inc(w_done[par], 1)
            group_pairs(dve, group_b)

            def block_c(i, par, b):
                dve.wait_ge(nd_in[par], 32 * (i + 1))
                den = nd[par][:, 1, :]
                dve.tensor_scalar(den, den, EPS_SUM, None, ALU.add).then_inc(nd_step[par], 1)
                dve.wait_ge(nd_step[par], 3 * i + 1)
                dve.reciprocal(den, den).then_inc(nd_step[par], 1)
                dve.wait_ge(nd_step[par], 3 * i + 2)
                dve.wait_ge(g_ps[par], 4 * i)
                dve.tensor_tensor(aggn[par], nd[par][:, 0, :].rearrange("q (n t) -> q t n", t=HT),
                                  den.rearrange("q (n t) -> q t n", t=HT), ALU.mult).then_inc(nd_step[par], 1)
                dve.wait_ge(out_done[par], 16 * i)
                dve.wait_ge(stat_step[1 - par], (2 * BT + 1) * (i + par))
                dve.wait_ge(x2_in[par], 16 * (i + 1))
                for m in range(BT // 2):
                    h, u = 2 * m // HT, 2 * m % HT
                    dve.wait_ge(g_ps[par], 4 * i + m + 1)
                    dve.scalar_tensor_tensor(hb[par][:, h, u:u + 2, :].rearrange("p t d -> p (t d)"), ps[4 + m % 2][:, :], ETA * LAM,
                                             xs[par][:, h, u:u + 2, :].rearrange("p t d -> p (t d)"),
                                             ALU.max, ALU.add).then_inc(h_done[par], 1)
                    dve.wait_ge(h_done[par], 4 * i + m + 1)
                    for t in (2 * m, 2 * m + 1):
                        dve.bn_stats(stats[:, t, :], hb[par][:, t // HT, t % HT, :]).then_inc(stat_step[par], 1)
                step = (2 * BT + 1) * i
                dve.wait_ge(stat_step[par], step + BT)
                passed(dve)
                for t in range(BT):
                    dve.bn_aggr(mv[par][:, t, :], stats[:, t, :]).then_inc(stat_step[par], 1)
                dve.wait_ge(stat_step[par], step + 2 * BT)
                dve.tensor_scalar(std[par][:, :], mv[par][:, :, 1], EPS_LN, None, ALU.add).then_inc(stat_step[par], 1)
                dve.wait_ge(std_done[par], i + 1)
                dve.reciprocal(rstd[par][:, :], std[par][:, :]).then_inc(norm_step[par], 1)
                dve.wait_ge(norm_step[par], 2 * i + 1)
                dve.scalar_tensor_tensor(nmr[par][:, :], mv[par][:, :, 0], -1.0, rstd[par][:, :], ALU.mult, ALU.mult
                                         ).then_inc(norm_step[par], 1)
            block_pairs(dve, block_c)


def kernel(x, src, dst, L0_gnn_U, L0_gnn_Dmat, L0_gnn_head_w):
    import numpy as np
    import concourse.bacc as bacc
    from concourse.bass_utils import run_bass_kernel_spmd

    nc = bacc.Bacc("TRN2", target_bir_lowering=False, num_devices=1)
    named = {"x": x, "src": src, "dst": dst, "U": L0_gnn_U, "Dmat": L0_gnn_Dmat, "head_w": L0_gnn_head_w}
    arrays, args = {}, []
    for name, a in named.items():
        a = np.ascontiguousarray(a)
        arrays[f"in_{name}"] = a
        args.append(nc.dram_tensor(f"in_{name}", a.shape, mybir.dt.from_np(a.dtype), kind="ExternalInput").ap())
    args.append(nc.dram_tensor("out", (N, D), mybir.dt.float32, kind="ExternalOutput").ap())
    build(nc, *args)
    r = run_bass_kernel_spmd(nc, [arrays], core_ids=[0])
    return r.results[0]["out"]
```

```python
import concourse.bass as bass
from concourse import mybir
from contextlib import ExitStack

N, D, K, R, E = 100000, 256, 4, 16, 125000
F = K * R
P = 128
HALVES = D // P
ETA, LAM, C = 0.5, 0.1, 0.5
EPS_SUM, EPS_LN = 1e-16, 1e-5
BIG = 1.0e38

BN = 1024
BT = BN // P
HB = BN // 2
HT = BT // 2
NBLOCKS = -(-N // BN)
LAST_BASE = N - BN
SLOTS = 4
BTURNS = NBLOCKS // SLOTS
BPAIRS = NBLOCKS // 2

ET = 125
TG = 25
GE = ET * TG
GROUPS = E // GE
GPAIRS = GROUPS // 2
TILES = GROUPS * TG
WIN = P
CT = 5
CHUNKS = TG // CT
KJ = K * TG
IQ = 8
ROW = -(-TG // 4) * 4
SPR = TG + 1


def build(nc, x, src, dst, U, Dmat, head_w, out):
    f32, i32 = mybir.dt.float32, mybir.dt.int32
    ALU, ACT, AX = mybir.AluOpType, mybir.ActivationFunctionType, mybir.AxisListType
    ctx = ExitStack()
    with ctx:
        def sb(name, shape, dt=f32):
            return ctx.enter_context(nc.sbuf_tensor(name, shape, dt))

        def sem(name):
            return ctx.enter_context(nc.semaphore(name))

        def sem4(name):
            return [sem(f"{name}{p}") for p in range(SLOTS)]

        def sem2(name):
            return [sem(f"{name}{p}") for p in range(2)]

        ps = [ctx.enter_context(nc.psum_tensor(f"bank{b}", [P, 512], f32)) for b in range(8)]

        z_dram = nc.dram_tensor("z_dram", [N + WIN, F], f32).ap()
        num_dram = nc.dram_tensor("num_dram", [F, N + GE], f32).ap()
        den_dram = nc.dram_tensor("den_dram", [K, N + GE], f32).ap()
        rden_dram = nc.dram_tensor("rden_dram", [K, N], f32).ap()
        dst_pad = nc.dram_tensor("dst_pad", [1, E + 2], i32).ap()

        ident = sb("ident", [P, P])
        iota_i = sb("iota_i", [P, P + 1], i32)
        iota_row = sb("iota_row", [P, P])
        iota_col = sb("iota_col", [P, 1])
        ones = sb("ones", [1, P])
        minus1 = sb("minus1", [1, 1], i32)
        U_sb = sb("U_sb", [P, HALVES, F])
        Uw = sb("Uw", [P, HALVES, 2, F])
        D_sb = sb("D_sb", [P, HALVES, D])
        DtD = sb("DtD", [P, HALVES, D])
        Mh = sb("Mh", [P, HALVES, D])
        G2 = sb("G2", [P, D])
        hw = sb("hw", [P, K])
        hwm = sb("hwm", [P, 1])
        hws = sb("hws", [P, 1])
        src_col = sb("src_col", [ET, TILES], i32)
        dst_col = sb("dst_col", [ET, TILES])
        first_all = sb("first_all", [P, TILES])
        node_col = sb("node_col", [P, TILES])
        dst_rel = sb("dst_rel", [ET, TILES])
        first_i = sb("first_i", [1, GROUPS, ROW], i32)
        off_i = sb("off_i", [1, GROUPS, ROW], i32)
        gap_i = sb("gap_i", [1, GROUPS], i32)
        xs = [sb(f"xs{p}", [P, 2, HT, D]) for p in range(2)]
        xT = [sb(f"xT{p}", [P, 2, HALVES, P]) for p in range(2)]
        zo = [sb(f"zo{s}", [P, 2, HT, F]) for s in range(SLOTS)]
        idx_g = [sb(f"idx_g{p}", [ET, TG], i32) for p in range(2)]
        zs = [sb(f"zs{p}", [ET, TG, F]) for p in range(2)]
        zw = [sb(f"zw{p}", [WIN, TG, F]) for p in range(2)]
        dst_b = [sb(f"dst_b{p}", [P, TG, ET], i32) for p in range(2)]
        rows_i = [sb(f"rows_i{p}", [KJ, ET + 2], i32) for p in range(2)]
        nodes_g = sb("nodes_g", [P, TG])
        rel_g = sb("rel_g", [ET, TG])
        spread = [sb(f"spread{p}", [WIN, CT, ET]) for p in range(2)]
        onehot = sb("onehot", [P, TG, WIN])
        prod = sb("prod", [ET, CT, K, R])
        logit = sb("logit", [ET, K, TG])
        rows = sb("rows", [KJ, ET + 2])
        pen = sb("pen", [KJ, ET + 1])
        pen_first = sb("pen_first", [KJ, ET])
        pen_last = sb("pen_last", [KJ, ET])
        fmax = sb("fmax", [KJ, ET])
        rmax = sb("rmax", [KJ, ET])
        m1 = sb("m1", [KJ, ET])
        m2 = sb("m2", [KJ, ET])
        shifted = sb("shifted", [KJ, ET])
        edge4 = sb("edge4", [1, 4, KJ])
        differ = sb("differ", [1, 2, KJ])
        fpen = sb("fpen", [1, K, SPR])
        bpen = sb("bpen", [1, K, SPR])
        fval = sb("fval", [1, K, SPR])
        bval = sb("bval", [1, K, SPR])
        run = sb("run", [1, K, SPR])
        back = sb("back", [1, K, SPR])
        beside = sb("beside", [1, 2, KJ])
        rrow = sb("rrow", [1, 2, K, R])
        rrow2 = sb("rrow2", [1, 2, K, R])
        rscale = sb("rscale", [P, 1])
        W = sb("W", [P, TG, 2, F])
        agg = [sb(f"agg{p}", [P, GE + WIN]) for p in range(2)]
        raw_i = onehot[:ET, :, :].rearrange("p t e -> p (t e)")[:, 0:2 * ET * IQ].bitcast(i32).rearrange("p (s c) -> p s c", s=2)
        raw_f = W[:ET, :, :, :].rearrange("p t a f -> p (t a f)")[:, 0:2 * ET * IQ].rearrange("p (s c) -> p s c", s=2)
        xs += [dst_b[p][:, :, :].rearrange("p t e -> p (t e)")[:, 0:BT * D].bitcast(f32).rearrange(
            "p (h t d) -> p h t d", h=2, t=HT) for p in range(2)]
        DN = N // (P // K)
        dens = agg[0][:, 0:DN]
        nd = [agg[p][:, 0:2 * HB].rearrange("q (a n) -> q a n", a=2) for p in range(2)]
        aggn = [agg[p][:, 2 * HB:3 * HB].rearrange("q (t n) -> q t n", t=HT) for p in range(2)]
        hb = [onehot[:, :, :].rearrange("p t n -> p (t n)")[:, 0:BT * D].rearrange("p (h t d) -> p h t d", h=2, t=HT),
              W[:, :, :, :].rearrange("p t a f -> p (t a f)")[:, 0:BT * D].rearrange("p (h t d) -> p h t d", h=2, t=HT)]
        stats = sb("stats", [P, BT, 6])
        mv = [sb(f"mv{p}", [P, BT, 2]) for p in range(2)]
        varm = [sb(f"varm{p}", [P, 2, BT]) for p in range(2)]
        minus_half = sb("minus_half", [P, BT])
        rstd = [sb(f"rstd{p}", [P, BT]) for p in range(2)]
        nmr = [sb(f"nmr{p}", [P, BT]) for p in range(2)]

        const_step = sem("const_step")
        w_in = sem("w_in")
        pad_out = sem("pad_out")
        idx_float = sem("idx_float")
        idx_ps = sem("idx_ps")
        idx_sb = sem("idx_sb")
        prep_pe = sem("prep_pe")
        prep_dve = sem("prep_dve")
        prep_act = sem("prep_act")
        gate = sem("gate")
        x_in = sem4("x_in")
        xt_ps = sem4("xt_ps")
        xt_sb = [sem(f"xt_sb{m}") for m in range(2)]
        xt_used = [sem(f"xt_used{m}") for m in range(2)]
        z_sb = sem2("z_sb")
        z_out = sem4("z_out")
        idx_ready = sem2("idx_ready")
        gathered = [[sem(f"gathered{p}_{c}") for c in range(CHUNKS)] for p in range(2)]
        zw_in = sem2("zw_in")
        rows_in = sem2("rows_in")
        cols_g = sem("cols_g")
        spread_done = sem2("spread_done")
        zd_ps = sem2("zd_ps")
        prod_done = sem2("prod_done")
        logit_done = sem2("logit_done")
        oh_done = sem("oh_done")
        flag_step = sem("flag_step")
        flag_ps = sem("flag_ps")
        lrow_ps = sem("lrow_ps")
        scan_step = sem("scan_step")
        ab_ps = sem("ab_ps")
        chain_step = sem("chain_step")
        li_ps = sem("li_ps")
        r_exp = sem("r_exp")
        r_ps = sem("r_ps")
        shifted_ps = sem("shifted_ps")
        p_done = sem("p_done")
        w_done = sem2("w_done")
        agg_ps = sem("agg_ps")
        agg_step = sem("agg_step")
        flushed = sem2("flushed")
        dens_in = sem("dens_in")
        rden_sb = sem("rden_sb")
        rden_out = sem("rden_out")
        x2_in = sem4("x2_in")
        nd_in = sem2("nd_in")
        quot = sem2("quot")
        xt2_ps = sem2("xt2_ps")
        xt2_sb = [sem(f"xt2_sb{m}") for m in range(2)]
        g_ps = sem2("g_ps")
        h_done = sem2("h_done")
        stat_step = sem2("stat_step")
        norm_step = sem2("norm_step")
        normed = sem2("normed")
        out_done = sem2("out_done")

        CONSTS = 14
        W_IN = 16 * 9
        PREP_IDX = 9
        PREP = 21
        FLAG, SCAN, CHAIN, AGG, STAT = 9, 5, 9, 2 + 2 * TG, 2 * BT + 2

        def block_base(b):
            return LAST_BASE if isinstance(b, int) and b == NBLOCKS - 1 else b * BN

        def block_rows(t, base):
            return t[bass.ds(base, BN), :].rearrange("(h p t) d -> p h (t d)", h=2, t=HT)

        def blocks(eng, body):
            def turn(i, slots):
                for s in range(slots):
                    body(i, s, s % 2, i * SLOTS + s, i * (SLOTS // 2) + s // 2)
            turn(0, SLOTS)
            with eng.Fori(1, BTURNS) as i:
                turn(i, SLOTS)
            turn(BTURNS, NBLOCKS - BTURNS * SLOTS)

        def group_pairs(eng, body):
            for par in range(2):
                body(0, par, par)
            with eng.Fori(1, GPAIRS) as i:
                for par in range(2):
                    body(i, par, i * 2 + par)

        def free(eng, sem_, value):
            if not isinstance(value, int) or value > 0:
                eng.wait_ge(sem_, value)

        def z_stored(eng):
            for s in range(SLOTS):
                eng.wait_ge(z_out[s], 16 * len(range(s, NBLOCKS, SLOTS)))

        def row_values(eng_type, table, g, limit):
            return nc.values_load_multi_w_load_instructions(
                table[0:1, bass.ds(g, 1), 0:TG].rearrange("a g t -> a (g t)"), engines=(eng_type,),
                min_val=0, max_val=limit)[1]

        def passed(eng):
            eng.sem_inc(gate, 1)

        block = ctx.enter_context(nc.Block())

        @block.sync
        def _(sp):
            for h in range(HALVES):
                sp.dma_start(U_sb[:, h, :].rearrange("p (k r) -> p k r", k=K),
                             U[:, h * P:(h + 1) * P, :].rearrange("k p r -> p k r")).then_inc(w_in, 16)
                sp.dma_start(D_sb[:, h, :], Dmat[h * P:(h + 1) * P, :]).then_inc(w_in, 16)
            sp.dma_start(hw[:, :], head_w.rearrange("(a k) -> a k", a=1).to_broadcast([P, K])).then_inc(w_in, 16)
            sp.dma_start(raw_i[:, 0, :], src.rearrange("(q c) -> q c", q=ET)).then_inc(w_in, 16)
            sp.dma_start(raw_i[:, 1, :], dst.rearrange("(q c) -> q c", q=ET)).then_inc(w_in, 16)
            sp.dma_start(dst_pad[0:1, 1:E + 1].rearrange("a (q c) -> (a q) c", q=ET),
                         dst.rearrange("(q c) -> q c", q=ET)).then_inc(pad_out, 16)
            sp.wait_ge(const_step, 3)
            sp.dma_start(dst_pad[0:1, 0:1], minus1[:, :]).then_inc(w_in, 16)
            sp.dma_start(dst_pad[0:1, E + 1:E + 2], minus1[:, :]).then_inc(w_in, 16)
            sp.wait_ge(const_step, 4)
            sp.dma_start(z_dram[N:N + WIN, :], agg[0][:, 0:F]).then_inc(pad_out, 16)

            def load_x(i, s, par, b, n):
                free(sp, xt_ps[s], 4 * i)
                sp.dma_start(xs[s][:, :, :, :].rearrange("p h t d -> p h (t d)"),
                             block_rows(x, block_base(b))).then_inc(x_in[s], 16)
                if isinstance(b, int) and b < SLOTS:
                    return
                store_z(i - 1, s, par, b - SLOTS, n - SLOTS // 2)

            def store_z(i, s, par, b, n):
                sp.wait_ge(z_sb[par], n + 1)
                if isinstance(b, int) and b == NBLOCKS - 1:
                    sp.wait_ge(z_out[(b - 1) % SLOTS], 16 * ((b - 1) // SLOTS + 1))
                sp.dma_start(z_dram[bass.ds(block_base(b), BN), :].rearrange("(h p t) f -> p h (t f)", h=2, t=HT),
                             zo[s][:, :, :, :].rearrange("p h t f -> p h (t f)")).then_inc(z_out[s], 16)
            blocks(sp, load_x)
            for b in range(NBLOCKS - SLOTS, NBLOCKS):
                store_z(b // SLOTS, b % SLOTS, b % 2, b, b // 2)

            sp.wait_ge(prep_dve, PREP_IDX)
            sp.wait_ge(pad_out, 32)
            sp.wait_ge(w_in, W_IN)
            z_stored(sp)

            def load_group(i, par, g):
                free(sp, spread_done[par], CHUNKS * i)
                sp.dma_start(dst_b[par][:, :, :].rearrange("p t e -> p (t e)"),
                             dst_pad[0:1, bass.ds(g * GE + 1, GE)].to_broadcast([P, GE])).then_inc(rows_in[par], 16)
                v = dst_pad[0:1, bass.ds(g * GE, GE)].rearrange("a (t e) -> (a t) e", t=TG)
                v = bass.AP(v.tensor, v.offset, [[ET, TG], [1, ET + 2]], runtime_checks=v.runtime_checks)
                for k in range(K):
                    sp.dma_start(rows_i[par][k * TG:(k + 1) * TG, :], v).then_inc(rows_in[par], 16)
                free(sp, zd_ps[par], CHUNKS * i)
                passed(sp)
                for t, n0 in enumerate(row_values(mybir.EngineType.SP, first_i, g, N - 1)):
                    sp.dma_start(zw[par][:, t, :], z_dram[bass.ds(n0, WIN), :]).then_inc(zw_in[par], 16)

            group_pairs(sp, load_group)

            for par in range(2):
                sp.wait_ge(flushed[par], 32 * GPAIRS)
            for k in range(K):
                sp.dma_start(dens[k * P // K:(k + 1) * P // K, :],
                             den_dram[k:k + 1, 0:N].rearrange("a (c n) -> (a c) n", n=DN)).then_inc(dens_in, 16)
            sp.wait_ge(rden_sb, 2)
            for k in range(K):
                sp.dma_start(rden_dram[k:k + 1, :].rearrange("a (c n) -> (a c) n", n=DN),
                             dens[k * P // K:(k + 1) * P // K, :]).then_inc(rden_out, 16)

            sp.wait_ge(rden_out, 16 * K)

            def load_c(i, s, par, b, n):
                base = block_base(b)
                free(sp, h_done[par], 4 * (n - 1))
                sp.dma_start(xs[s][:, :, :, :].rearrange("p h t d -> p h (t d)"),
                             block_rows(x, base)).then_inc(x2_in[s], 16)
                free(sp, quot[par], n)
                passed(sp)
                for h in range(2):
                    cols = bass.ds(base + h * HB, HB)
                    sp.dma_start(nd[par][h * F:(h + 1) * F, 0, :], num_dram[:, cols]).then_inc(nd_in[par], 16)
                    for k in range(K):
                        p0 = h * F + k * R
                        sp.dma_start(nd[par][p0:p0 + R, 1, :], rden_dram[k:k + 1, cols].to_broadcast([R, HB])
                                     ).then_inc(nd_in[par], 16)
            blocks(sp, load_c)
            for par in range(2):
                sp.wait_ge(out_done[par], 16 * BPAIRS)

        @block.gpsimd
        def _(pool):
            pool.memset(ident[:, :], 0.0).then_inc(const_step, 1)
            pool.memset(ones[:, :], 1.0).then_inc(const_step, 1)
            pool.memset(minus1[:, :], -1).then_inc(const_step, 1)
            pool.memset(agg[0][:, :], 0.0).then_inc(const_step, 1)
            pool.memset(agg[1][:, :], 0.0).then_inc(const_step, 1)
            pool.iota(iota_i[:, 0:P], [[1, P]], base=0, channel_multiplier=0).then_inc(const_step, 1)
            pool.iota(iota_i[:, P:P + 1], [[0, 1]], base=0, channel_multiplier=1).then_inc(const_step, 1)
            pool.wait_ge(const_step, 7)
            pool.affine_select(out=ident[:, :], in_=ident[:, :], compare_op=ALU.not_equal, fill=1.0,
                               base=0, pattern=[[-1, P]], channel_multiplier=1).then_inc(const_step, 1)
            pool.memset(fpen[:, :, 0:1], -BIG).then_inc(const_step, 1)
            pool.memset(bpen[:, :, TG:SPR], -BIG).then_inc(const_step, 1)
            pool.memset(bval[:, :, TG:SPR], -BIG).then_inc(const_step, 1)
            pool.memset(run[:, :, :], -BIG).then_inc(const_step, 1)
            pool.memset(gap_i[:, 0:1], 0).then_inc(const_step, 1)
            pool.memset(minus_half[:, :], -0.5).then_inc(const_step, 1)

            pool.wait_ge(prep_dve, PREP_IDX)
            z_stored(pool)

            def gather(i, par, g):
                for c in range(CHUNKS):
                    free(pool, gathered[par][c], i * CT * 16)
                pool.tensor_copy(idx_g[par][:, :], src_col[:, bass.ds(g * TG, TG)]).then_inc(idx_ready[par], 1)
                free(pool, w_done[par], i)
                pool.wait_ge(idx_ready[par], i + 1)
                passed(pool)
                for t in range(TG):
                    pool.indirect_dma_start(
                        out=zs[par][:, t, :], out_offset=None, in_=z_dram[:, :],
                        in_offset=bass.IndirectOffsetOnAxis(ap=idx_g[par][:, t:t + 1], axis=0),
                        ).then_inc(gathered[par][t // CT], 16)
            group_pairs(pool, gather)

            def normalise(i, s, par, b, n):
                pool.wait_ge(stat_step[par], STAT * (n + 1))
                free(pool, normed[par], BT * n)
                pool.tensor_tensor(rstd[par][:, :], varm[par][:, 0, :], minus_half[:, :], ALU.pow
                                   ).then_inc(norm_step[par], 1)
                pool.wait_ge(norm_step[par], 2 * n + 1)
                pool.tensor_tensor(nmr[par][:, :], varm[par][:, 1, :], rstd[par][:, :], ALU.mult
                                   ).then_inc(norm_step[par], 1)
                pool.wait_ge(norm_step[par], 2 * n + 2)
                passed(pool)
                for t in range(BT):
                    h, u = t // HT, t % HT
                    pool.tensor_scalar(hb[par][:, h, u, :], hb[par][:, h, u, :],
                                       rstd[par][:, t:t + 1], nmr[par][:, t:t + 1], ALU.mult, ALU.add
                                       ).then_inc(normed[par], 1)
                pool.wait_ge(normed[par], BT * (n + 1))
                if isinstance(b, int) and b == NBLOCKS - 1:
                    pool.wait_ge(out_done[0], 16 * BPAIRS)
                pool.dma_start(block_rows(out, block_base(b)),
                               hb[par][:, :, :, :].rearrange("p h t d -> p h (t d)")).then_inc(out_done[par], 16)
            blocks(pool, normalise)

        @block.tensor
        def _(pe):
            pe.wait_ge(const_step, CONSTS)
            n = 0
            for s in range(2):
                for c in range(IQ):
                    pe.wait_ge(idx_float, 2)
                    if n >= 2:
                        pe.wait_ge(idx_sb, n - 1)
                    pe.transpose(ps[n % 2][:ET, 0:ET], raw_f[:, s, c * ET:(c + 1) * ET],
                                 ident[:ET, :ET]).then_inc(idx_ps, 1)
                    n += 1
            pe.wait_ge(idx_sb, 2 * IQ)
            for c in range(2):
                pe.matmul(ps[2 + c][:, 0:TILES // 2], ones[:, :], dst_col[0:1, c * TILES // 2:(c + 1) * TILES // 2],
                          start=True, stop=True).then_inc(prep_pe, 1)
            pe.wait_ge(w_in, W_IN)
            for a in range(HALVES):
                for b in range(HALVES):
                    mm = pe.matmul(ps[4 + a][:, 0:D], D_sb[:, b, a * P:(a + 1) * P], D_sb[:, b, :],
                                   start=b == 0, stop=b == HALVES - 1)
                mm.then_inc(prep_pe, 1)
            pe.wait_ge(prep_act, 3)
            for a in range(HALVES):
                for b in range(HALVES):
                    mm = pe.matmul(ps[6 + a][:, 0:D], DtD[:, b, a * P:(a + 1) * P], D_sb[:, b, :],
                                   start=b == 0, stop=b == HALVES - 1)
                mm.then_inc(prep_pe, 1)
            pe.wait_ge(prep_dve, PREP)
            for h in range(HALVES):
                mm = pe.matmul(ps[4][:, 0:D], Uw[:, h, :, :].rearrange("p a f -> p (a f)"), Mh[:, h, :],
                               start=h == 0, stop=h == HALVES - 1)
            mm.then_inc(prep_pe, 1)

            def transposes(m, x_sb, ps_sem):
                for u in range(2):
                    t = 2 * m + u
                    for h in range(HALVES):
                        tr = pe.transpose(ps[m % 2][:, (u * HALVES + h) * P:(u * HALVES + h + 1) * P],
                                          x_sb[:, t // HT, t % HT, h * P:(h + 1) * P], ident[:, :])
                tr.then_inc(ps_sem, 1)

            def block_a(i, s, par, b, n):
                pe.wait_ge(x_in[s], 16 * (i + 1))

                def zmm(m):
                    pe.wait_ge(xt_sb[m % 2], 2 * b + m // 2 + 1)
                    if m == 0:
                        free(pe, z_sb[par], n)
                    for u in range(2):
                        t = 2 * m + u
                        for h in range(HALVES):
                            mm = pe.matmul(ps[2 + par][:, t * F:(t + 1) * F], xT[m % 2][:, u, h, :], U_sb[:, h, :],
                                           start=h == 0, stop=h == HALVES - 1)
                    mm.then_inc(xt_used[m % 2], 1)
                for m in range(BT // 2):
                    free(pe, xt_sb[m % 2], 2 * b + m // 2)
                    transposes(m, xs[s], xt_ps[s])
                    if m:
                        zmm(m - 1)
                zmm(BT // 2 - 1)
            blocks(pe, block_a)

            def group_b(i, par, g):
                pe.wait_ge(flag_step, FLAG * g + 1)
                for n, c in enumerate((0, 1, ET, ET + 1)):
                    tr = pe.transpose(ps[6][0:1, n * KJ:(n + 1) * KJ], rows[:, c:c + 1], ident[:KJ, :KJ])
                tr.then_inc(flag_ps, 1)
                pe.wait_ge(zw_in[par], (i + 1) * TG * 16)
                for c in range(CHUNKS):
                    pe.wait_ge(spread_done[par], i * CHUNKS + c + 1)
                    if c >= 2:
                        pe.wait_ge(prod_done[par], i * CHUNKS + c - 1)
                    else:
                        free(pe, prod_done[1 - par], (i + par) * CHUNKS)
                    for u in range(CT):
                        mm = pe.matmul(ps[2 + c % 2][:ET, u * F:(u + 1) * F], spread[c % 2][:, u, :],
                                       zw[par][:, c * CT + u, :], start=True, stop=True)
                    mm.then_inc(zd_ps[par], 1)
                pe.wait_ge(logit_done[par], (i + 1) * CHUNKS)
                pe.transpose(ps[4][:KJ, 0:ET], logit[:, :, :].rearrange("p k t -> p (k t)"),
                             ident[:ET, :ET]).then_inc(lrow_ps, 1)
                pe.wait_ge(scan_step, SCAN * g + 2)
                pe.transpose(ps[6][0:1, 0:KJ], rmax[:, 0:1], ident[:KJ, :KJ])
                pe.transpose(ps[6][0:1, KJ:2 * KJ], rmax[:, ET - 1:ET], ident[:KJ, :KJ]).then_inc(ab_ps, 1)
                pe.wait_ge(chain_step, CHAIN * g + 7)
                pe.matmul(ps[7][:KJ, 0:1], beside[:, 0, :], ones[:, 0:1], start=True, stop=True)
                pe.matmul(ps[7][:KJ, 1:2], beside[:, 1, :], ones[:, 0:1], start=True, stop=True).then_inc(li_ps, 1)
                pe.wait_ge(r_exp, g + 1)
                pe.matmul(ps[5][:, KJ:KJ + 1], rrow2[0:1, :, :, :].rearrange("a b k r -> a (b k r)"), ones[:, 0:1],
                          start=True, stop=True).then_inc(r_ps, 1)
                pe.wait_ge(scan_step, SCAN * g + 5)
                pe.transpose(ps[5][:ET, 0:KJ], shifted[:, :], ident[:KJ, :KJ]).then_inc(shifted_ps, 1)
                pe.wait_ge(w_done[par], i + 1)
                pe.wait_ge(oh_done, g + 1)
                for t in range(TG):
                    q = t // 4
                    if t % 4 == 0:
                        free(pe, agg_step, g * AGG + (2 + 8 * (q - 1) if q >= 2 else 0))
                    pe.matmul(ps[q % 2][:, (t % 4) * P:(t % 4 + 1) * P], W[:ET, t, :, :].rearrange("p a f -> p (a f)"),
                              onehot[:ET, t, :], start=True, stop=True).then_inc(agg_ps, 1)
            group_pairs(pe, group_b)

            def block_c(i, s, par, b, n):
                pe.wait_ge(x2_in[s], 16 * (i + 1))

                def gmm(m):
                    pe.wait_ge(xt2_sb[m % 2], 2 * b + m // 2 + 1)
                    if m == 0:
                        pe.wait_ge(quot[par], n + 1)
                    if m >= 2:
                        pe.wait_ge(h_done[par], 4 * n + m - 1)
                    else:
                        free(pe, h_done[1 - par], 4 * (n + par))
                    for u in range(2):
                        t = 2 * m + u
                        hf, uu = t // HT, t % HT
                        o = ps[4 + m % 2][:, u * D:(u + 1) * D]
                        for h in range(HALVES):
                            pe.matmul(o, xT[m % 2][:, u, h, :], Mh[:, h, :], start=h == 0, stop=False)
                        mm = pe.matmul(o, aggn[par][hf * F:(hf + 1) * F, uu, :], G2[hf * F:(hf + 1) * F, :],
                                       start=False, stop=True)
                    mm.then_inc(g_ps[par], 1)
                for m in range(BT // 2):
                    free(pe, xt2_sb[m % 2], 2 * b + m // 2)
                    transposes(m, xs[s], xt2_ps[par])
                    if m:
                        gmm(m - 1)
                gmm(BT // 2 - 1)
            blocks(pe, block_c)

        @block.scalar
        def _(act):
            act.wait_ge(prep_dve, PREP_IDX + 2)
            act.activation(hw[:, :], hw[:, :], ACT.Exp, bias=hwm[:, :], accum_out=hws[:, :]).then_inc(prep_act, 1)
            for a in range(HALVES):
                act.wait_ge(prep_pe, 3 + a)
                act.activation(DtD[:, a, :], ps[4 + a][:, 0:D], ACT.Copy).then_inc(prep_act, 1)
            act.wait_ge(prep_pe, 7)
            act.activation(G2[:, :], ps[4][:, 0:D], ACT.Copy).then_inc(prep_act, 1)

            def block_a(i, s, par, b, n):
                for m in range(1, BT // 2, 2):
                    act.wait_ge(xt_ps[s], 4 * i + m + 1)
                    free(act, xt_used[1], 2 * b + m // 2)
                    act.activation(xT[1][:, :, :, :].rearrange("p u h n -> p (u h n)"), ps[1][:, :], ACT.Copy
                                   ).then_inc(xt_sb[1], 1)
                if par == 1:
                    act.wait_ge(xt_used[1], 2 * b + 2)
                    free(act, z_out[s], 16 * i)
                    act.activation(zo[s][:, :, :, :].rearrange("p h t f -> p (h t f)"), ps[3][:, :], ACT.Copy
                                   ).then_inc(z_sb[1], 1)
            blocks(act, block_a)

            def group_b(i, par, g):
                act.wait_ge(chain_step, CHAIN * g + 9)
                free(act, r_ps, g)
                act.activation(rrow2[:, :, :, :].rearrange("a b k r -> a (b k r)"),
                               rrow[:, :, :, :].rearrange("a b k r -> a (b k r)"), ACT.Exp).then_inc(r_exp, 1)
                act.wait_ge(shifted_ps, g + 1)
                free(act, agg_ps, g * TG)
                act.activation(W[:ET, :, 1, :].rearrange("p t (k r) -> p t k r", k=K),
                               ps[5][:ET, 0:KJ].rearrange("p (k t) -> p t k", k=K).unsqueeze(3).to_broadcast([ET, TG, K, R]),
                               ACT.Exp).then_inc(p_done, 1)
                act.wait_ge(r_ps, g + 1)
                free(act, agg_step, g * AGG)
                act.activation(rscale[:, :], ps[5][:, KJ:KJ + 1], ACT.Copy).then_inc(agg_step, 1)
                act.wait_ge(agg_step, g * AGG + 1)
                free(act, flushed[par], 32 * i)
                gap = act.value_load(gap_i[0:1, bass.ds(g, 1)], min_val=0, max_val=GE)
                act.activation(agg[par][:, 0:1], agg[1 - par][:, bass.ds(gap, 1)], ACT.Copy, scale=rscale[:, :]
                               ).then_inc(agg_step, 1)
                offs = row_values(mybir.EngineType.Activation, off_i, g, GE - 1)
                for t in range(TG):
                    bank = ps[(t // 4) % 2]
                    off = offs[t]
                    if t % 4 == 0:
                        act.wait_ge(agg_ps, g * TG + min(t + 4, TG))
                    act.wait_ge(agg_step, g * AGG + 2 + 2 * t)
                    col = agg[par][:, bass.ds(off, 1)]
                    act.activation(col, bank[:, (t % 4) * P:(t % 4) * P + 1], ACT.Identity, bias=col
                                   ).then_inc(agg_step, 1)
                    act.activation(agg[par][:, bass.ds(off + 1, WIN - 1)], bank[:, (t % 4) * P + 1:(t % 4 + 1) * P],
                                   ACT.Copy).then_inc(agg_step, 1)
                n0 = act.value_load(first_i[0:1, bass.ds(g, 1), 0:1].rearrange("a g t -> a (g t)"), min_val=0, max_val=N - 1)
                act.wait_ge(agg_step, (g + 1) * AGG)
                free(act, flushed[1 - par], 32 * (i + par))
                act.dma_start(num_dram[:, bass.ds(n0, GE)], agg[par][0:F, 0:GE]).then_inc(flushed[par], 16)
                act.dma_start(den_dram[:, bass.ds(n0, GE)], agg[par][F:2 * F:R, 0:GE]).then_inc(flushed[par], 16)
            group_pairs(act, group_b)

            def block_c(i, s, par, b, n):
                for m in range(BT // 2):
                    act.wait_ge(xt2_ps[par], 4 * n + m + 1)
                    if m >= 2:
                        act.wait_ge(g_ps[par], 4 * n + m - 1)
                    else:
                        free(act, g_ps[1 - par], 4 * (n + par))
                    act.activation(xT[m % 2][:, :, :, :].rearrange("p u h n -> p (u h n)"), ps[m % 2][:, :], ACT.Copy
                                   ).then_inc(xt2_sb[m % 2], 1)
            blocks(act, block_c)

        @block.vector
        def _(dve):
            dve.wait_ge(const_step, CONSTS)
            dve.tensor_copy(iota_row[:, :], iota_i[:, 0:P]).then_inc(prep_dve, 1)
            dve.tensor_copy(iota_col[:, :], iota_i[:, P:P + 1]).then_inc(prep_dve, 1)
            dve.wait_ge(w_in, W_IN)
            dve.tensor_copy(raw_f[:, 0, :], raw_i[:, 0, :]).then_inc(idx_float, 1)
            dve.tensor_copy(raw_f[:, 1, :], raw_i[:, 1, :]).then_inc(idx_float, 1)
            n = 0
            for col in (src_col, dst_col):
                for c in range(IQ):
                    dve.wait_ge(idx_ps, n + 1)
                    dve.tensor_copy(col[:, :].rearrange("p (q j) -> p j q", j=IQ)[:, c, :], ps[n % 2][:ET, 0:ET]
                                    ).then_inc(idx_sb, 1)
                    n += 1
            for c in range(2):
                half = slice(c * TILES // 2, (c + 1) * TILES // 2)
                dve.wait_ge(prep_pe, 1 + c)
                dve.tensor_copy(first_all[:, half], ps[2 + c][:, 0:TILES // 2]).then_inc(prep_dve, 1)
            dve.wait_ge(prep_dve, 4)
            dve.tensor_scalar(node_col[:, :], first_all[:, :], iota_col[:, :], None, ALU.add).then_inc(prep_dve, 1)
            dve.tensor_tensor(dst_rel[:, :], dst_col[:, :], first_all[:ET, :], ALU.subtract).then_inc(prep_dve, 1)
            by_group = first_all[0:1, :].rearrange("a (g t) -> a g t", t=TG)
            dve.tensor_copy(first_i[:, :, 0:TG], by_group).then_inc(prep_dve, 1)
            dve.tensor_tensor(off_i[:, :, 0:TG], by_group,
                              by_group[:, :, 0:1].to_broadcast([1, GROUPS, TG]), ALU.subtract).then_inc(prep_dve, 1)
            dve.tensor_tensor(gap_i[:, 1:GROUPS], by_group[:, 1:GROUPS, 0], by_group[:, 0:GROUPS - 1, 0],
                              ALU.subtract).then_inc(prep_dve, 1)

            dve.tensor_reduce(hwm[:, :], hw[:, :], AX.X, ALU.max).then_inc(prep_dve, 1)
            dve.wait_ge(prep_dve, PREP_IDX + 1)
            dve.tensor_scalar(hwm[:, :], hwm[:, :], -1.0, None, ALU.mult).then_inc(prep_dve, 1)
            dve.wait_ge(prep_act, 1)
            dve.reciprocal(hws[:, :], hws[:, :]).then_inc(prep_dve, 1)
            dve.wait_ge(prep_dve, PREP_IDX + 3)
            dve.tensor_scalar(hw[:, :], hw[:, :], hws[:, :], None, ALU.mult).then_inc(prep_dve, 1)
            dve.wait_ge(prep_dve, PREP_IDX + 4)
            for a in range(2):
                dve.tensor_tensor(Uw[:, :, a, :].rearrange("p h (k r) -> p h k r", k=K),
                                  U_sb[:, :, :].rearrange("p h (k r) -> p h k r", k=K),
                                  hw[:, :].unsqueeze(1).unsqueeze(3).to_broadcast([P, HALVES, K, R]), ALU.mult
                                  ).then_inc(prep_dve, 1)
            for a in range(HALVES):
                dve.wait_ge(prep_pe, 5 + a)
                dve.tensor_tensor(Mh[:, a, :], D_sb[:, a, :], ps[6 + a][:, 0:D], ALU.subtract).then_inc(prep_dve, 1)
            dve.wait_ge(prep_dve, PREP_IDX + 8)
            for a in range(HALVES):
                dve.tensor_scalar(Mh[:, a, :], Mh[:, a, :], C * ETA, None, ALU.mult).then_inc(prep_dve, 1)
            dve.wait_ge(prep_dve, PREP_IDX + 10)
            for a in range(HALVES):
                diag = Mh[:, a, a * P:(a + 1) * P]
                dve.scalar_tensor_tensor(diag, ident[:, :], C, diag, ALU.mult, ALU.add).then_inc(prep_dve, 1)

            def block_a(i, s, par, b, n):
                for m in range(0, BT // 2, 2):
                    dve.wait_ge(xt_ps[s], 4 * i + m + 1)
                    free(dve, xt_used[0], 2 * b + m // 2)
                    dve.tensor_copy(xT[0][:, :, :, :].rearrange("p u h n -> p (u h n)"), ps[0][:, :]
                                    ).then_inc(xt_sb[0], 1)
                if par == 0:
                    dve.wait_ge(xt_used[1], 2 * b + 2)
                    free(dve, z_out[s], 16 * i)
                    dve.tensor_copy(zo[s][:, :, :, :].rearrange("p h t f -> p (h t f)"), ps[2][:, :]
                                    ).then_inc(z_sb[0], 1)
            blocks(dve, block_a)

            def group_b(i, par, g):
                flag, scan, chain = FLAG * g, SCAN * g, CHAIN * g
                free(dve, spread_done[1 - par], (i + par) * CHUNKS)
                free(dve, oh_done, g)
                free(dve, flag_step, flag)
                free(dve, scan_step, scan)
                free(dve, chain_step, chain)
                dve.tensor_copy(nodes_g[:, :], node_col[:, bass.ds(g * TG, TG)]).then_inc(cols_g, 1)
                dve.tensor_copy(rel_g[:, :], dst_rel[:, bass.ds(g * TG, TG)]).then_inc(cols_g, 1)
                dve.wait_ge(rows_in[par], 16 * (K + 1) * (i + 1))
                free(dve, flag_ps, g)
                dve.tensor_copy(rows[:, :], rows_i[par][:, :]).then_inc(flag_step, 1)
                dve.wait_ge(flag_step, flag + 1)
                dve.tensor_tensor(pen[:, :], rows[:, 1:ET + 2], rows[:, 0:ET + 1], ALU.not_equal).then_inc(flag_step, 1)
                dve.tensor_scalar(pen_first[:, :], rows[:, 1:ET + 1], rows[:, 0:1], -BIG, ALU.not_equal, ALU.mult
                                  ).then_inc(flag_step, 1)
                dve.tensor_scalar(pen_last[:, :], rows[:, 1:ET + 1], rows[:, ET + 1:ET + 2], -BIG,
                                  ALU.not_equal, ALU.mult).then_inc(flag_step, 1)
                dve.wait_ge(flag_step, flag + 2)
                dve.tensor_scalar(pen[:, :], pen[:, :], -BIG, None, ALU.mult).then_inc(flag_step, 1)

                def spreads(c):
                    if c == 0:
                        dve.wait_ge(cols_g, 2 * (g + 1))
                    if c >= 2:
                        dve.wait_ge(zd_ps[par], i * CHUNKS + c - 1)
                    else:
                        free(dve, zd_ps[1 - par], (i + par) * CHUNKS)
                    for u in range(CT):
                        t = c * CT + u
                        last = dve.tensor_scalar(spread[c % 2][:, u, :], dst_b[par][:, t, :], nodes_g[:, t:t + 1],
                                                 None, ALU.is_equal)
                    last.then_inc(spread_done[par], 1)

                def logits(c):
                    dve.wait_ge(zd_ps[par], i * CHUNKS + c + 1)
                    dve.wait_ge(gathered[par][c], 16 * CT * (i + 1))
                    if c == 0:
                        free(dve, lrow_ps, g)
                        free(dve, logit_done[1 - par], (i + par) * CHUNKS)
                    else:
                        dve.wait_ge(logit_done[par], i * CHUNKS + c)
                    dve.scalar_tensor_tensor(prod[:, :, :, :].rearrange("p t k r -> p (t k r)"),
                                             ps[2 + c % 2][:ET, 0:CT * F], float(R) ** -0.5,
                                             zs[par][:, c * CT:(c + 1) * CT, :].rearrange("p t f -> p (t f)"),
                                             ALU.mult, ALU.mult).then_inc(prod_done[par], 1)
                    dve.wait_ge(prod_done[par], i * CHUNKS + c + 1)
                    dve.tensor_reduce(logit[:, :, c * CT:(c + 1) * CT].rearrange("p k t -> p t k"),
                                      prod[:, :, :, :], AX.X, ALU.add).then_inc(logit_done[par], 1)

                def onehots(a, b):
                    if a == 0:
                        free(dve, agg_ps, g * TG)
                    for t in range(a, b):
                        last = dve.tensor_scalar(onehot[:ET, t, :], iota_row[:ET, :], rel_g[:, t:t + 1], None, ALU.is_equal)
                    if b == TG:
                        last.then_inc(oh_done, 1)

                spreads(0)
                spreads(1)
                for c in range(CHUNKS):
                    logits(c)
                    if c + 2 < CHUNKS:
                        spreads(c + 2)
                dve.wait_ge(flag_ps, g + 1)
                dve.tensor_copy(edge4[:, :, :].rearrange("a n k -> a (n k)"), ps[6][0:1, 0:4 * KJ]).then_inc(flag_step, 1)
                dve.tensor_copy(fval[:, :, 0:1], run[:, :, TG:SPR]).then_inc(chain_step, 1)
                onehots(0, 5)
                dve.wait_ge(flag_step, flag + 6)
                dve.tensor_tensor(differ[:, :, :], edge4[:, 0:2, :], edge4[:, 2:4, :], ALU.not_equal).then_inc(flag_step, 1)
                dve.wait_ge(lrow_ps, g + 1)
                dve.wait_ge(flag_step, flag + 7)
                dve.tensor_tensor_scan(fmax[:, :], pen[:, 0:ET], ps[4][:KJ, 0:ET], -BIG, ALU.add, ALU.max
                                       ).then_inc(scan_step, 1)
                dve.tensor_scalar(fpen[:, :, 1:SPR], differ[:, 0, :].rearrange("a (k t) -> a k t", k=K), -BIG, None,
                                  ALU.mult).then_inc(flag_step, 1)
                dve.tensor_scalar(bpen[:, :, 0:TG], differ[:, 1, :].rearrange("a (k t) -> a k t", k=K), -BIG, None,
                                  ALU.mult).then_inc(flag_step, 1)
                dve.wait_ge(scan_step, scan + 1)
                dve.tensor_tensor_scan(rmax[:, ::-1], pen[:, ET:0:-1], fmax[:, ::-1], -BIG, ALU.add, ALU.max
                                       ).then_inc(scan_step, 1)
                onehots(5, 10)
                dve.wait_ge(ab_ps, g + 1)
                dve.tensor_copy(bval[:, :, 0:TG], ps[6][0:1, 0:KJ].rearrange("a (k t) -> a k t", k=K)).then_inc(chain_step, 1)
                dve.tensor_copy(fval[:, :, 1:SPR], ps[6][0:1, KJ:2 * KJ].rearrange("a (k t) -> a k t", k=K)
                                ).then_inc(chain_step, 1)
                dve.wait_ge(chain_step, chain + 3)
                dve.wait_ge(flag_step, flag + 9)

                def flat(v):
                    return v[:, :, :].rearrange("a k s -> a (k s)")
                dve.tensor_tensor_scan(flat(run), flat(fpen), flat(fval), -BIG, ALU.add, ALU.max).then_inc(chain_step, 1)
                dve.tensor_tensor_scan(flat(back)[:, ::-1], flat(bpen)[:, ::-1], flat(bval)[:, ::-1], -BIG,
                                       ALU.add, ALU.max).then_inc(chain_step, 1)
                dve.wait_ge(chain_step, chain + 5)
                dve.tensor_copy(beside[:, 0, :].rearrange("a (k t) -> a k t", k=K), run[:, :, 0:TG]).then_inc(chain_step, 1)
                dve.tensor_copy(beside[:, 1, :].rearrange("a (k t) -> a k t", k=K), back[:, :, 1:SPR]).then_inc(chain_step, 1)
                free(dve, r_exp, g)
                dve.tensor_tensor(rrow[:, :, :, :], fval[:, :, 0:1].unsqueeze(1).to_broadcast([1, 2, K, R]),
                                  back[:, :, 0:1].unsqueeze(1).to_broadcast([1, 2, K, R]), ALU.subtract).then_inc(chain_step, 1)
                dve.wait_ge(chain_step, chain + 8)
                dve.tensor_scalar(rrow[:, :, :, :], rrow[:, :, :, :], 0.0, None, ALU.min).then_inc(chain_step, 1)
                onehots(10, 15)
                dve.wait_ge(li_ps, g + 1)
                dve.scalar_tensor_tensor(m1[:, :], pen_first[:, :], ps[7][:KJ, 0:1], rmax[:, :], ALU.add, ALU.max
                                         ).then_inc(scan_step, 1)
                dve.wait_ge(scan_step, scan + 3)
                dve.scalar_tensor_tensor(m2[:, :], pen_last[:, :], ps[7][:KJ, 1:2], m1[:, :], ALU.add, ALU.max
                                         ).then_inc(scan_step, 1)
                dve.wait_ge(scan_step, scan + 4)
                dve.tensor_tensor(shifted[:, :], ps[4][:KJ, 0:ET], m2[:, :], ALU.subtract).then_inc(scan_step, 1)
                onehots(15, TG)
                dve.wait_ge(p_done, g + 1)
                dve.tensor_tensor(W[:ET, :, 0, :], zs[par][:, :, :], W[:ET, :, 1, :], ALU.mult).then_inc(w_done[par], 1)
            group_pairs(dve, group_b)

            dve.wait_ge(dens_in, 16 * K)
            dve.tensor_scalar(dens, dens, EPS_SUM, None, ALU.add).then_inc(rden_sb, 1)
            dve.wait_ge(rden_sb, 1)
            dve.reciprocal(dens, dens).then_inc(rden_sb, 1)

            def quotients(par, n):
                dve.wait_ge(nd_in[par], 16 * 2 * (K + 1) * (n + 1))
                free(dve, g_ps[par], 4 * n)
                dve.tensor_tensor(aggn[par], nd[par][:, 0, :].rearrange("q (n t) -> q t n", t=HT),
                                  nd[par][:, 1, :].rearrange("q (n t) -> q t n", t=HT), ALU.mult).then_inc(quot[par], 1)

            def block_c(i, s, par, b, n):
                if not (isinstance(b, int) and b == NBLOCKS - 1):
                    quotients(1 - par, n + par)
                free(dve, out_done[par], 16 * n)
                free(dve, stat_step[1 - par], STAT * (n + par))
                for m in range(BT // 2):
                    h, u = 2 * m // HT, 2 * m % HT
                    dve.wait_ge(g_ps[par], 4 * n + m + 1)
                    dve.scalar_tensor_tensor(hb[par][:, h, u:u + 2, :].rearrange("p t d -> p (t d)"), ps[4 + m % 2][:, :],
                                             ETA * LAM, xs[s][:, h, u:u + 2, :].rearrange("p t d -> p (t d)"),
                                             ALU.max, ALU.add).then_inc(h_done[par], 1)
                    dve.wait_ge(h_done[par], 4 * n + m + 1)
                    for t in (2 * m, 2 * m + 1):
                        dve.bn_stats(stats[:, t, :], hb[par][:, t // HT, t % HT, :]).then_inc(stat_step[par], 1)
                dve.wait_ge(stat_step[par], STAT * n + BT)
                passed(dve)
                for t in range(BT):
                    dve.bn_aggr(mv[par][:, t, :], stats[:, t, :]).then_inc(stat_step[par], 1)
                dve.wait_ge(stat_step[par], STAT * n + 2 * BT)
                free(dve, norm_step[par], 2 * n)
                dve.tensor_scalar(varm[par][:, 0, :], mv[par][:, :, 1], EPS_LN, None, ALU.add).then_inc(stat_step[par], 1)
                dve.tensor_scalar(varm[par][:, 1, :], mv[par][:, :, 0], -1.0, None, ALU.mult).then_inc(stat_step[par], 1)
            quotients(0, 0)
            blocks(dve, block_c)


def kernel(x, src, dst, L0_gnn_U, L0_gnn_Dmat, L0_gnn_head_w):
    import numpy as np
    import concourse.bacc as bacc
    from concourse.bass_utils import run_bass_kernel_spmd

    nc = bacc.Bacc("TRN2", target_bir_lowering=False, num_devices=1)
    named = {"x": x, "src": src, "dst": dst, "U": L0_gnn_U, "Dmat": L0_gnn_Dmat, "head_w": L0_gnn_head_w}
    arrays, args = {}, []
    for name, a in named.items():
        a = np.ascontiguousarray(a)
        arrays[f"in_{name}"] = a
        args.append(nc.dram_tensor(f"in_{name}", a.shape, mybir.dt.from_np(a.dtype), kind="ExternalInput").ap())
    args.append(nc.dram_tensor("out", (N, D), mybir.dt.float32, kind="ExternalOutput").ap())
    build(nc, *args)
    r = run_bass_kernel_spmd(nc, [arrays], core_ids=[0])
    return r.results[0]["out"]
```

```python
import concourse.bass as bass
from concourse import mybir
from contextlib import ExitStack

N, D, K, R, E = 100000, 256, 4, 16, 125000
F = K * R
P = 128
HALVES = D // P
ETA, LAM, C = 0.5, 0.1, 0.5
EPS_SUM, EPS_LN = 1e-16, 1e-5
BIG = 1.0e38

BN = 1024
BT = BN // P
HB = BN // 2
HT = BT // 2
NBLOCKS = -(-N // BN)
LAST_BASE = N - BN
SLOTS = 4
BTURNS = NBLOCKS // SLOTS

ET = 125
TG = 25
GE = ET * TG
GROUPS = E // GE
GPAIRS = GROUPS // 2
TILES = GROUPS * TG
WIN = P
CT = 5
CHUNKS = TG // CT
KJ = K * TG
GB = GE // BN
TB = 2 * GB
XB = 3
PLAIN = 5
assert all(GE * (g - 1) - (E - N) >= BN * GB * (g - 2 * PLAIN + 1) for g in range(2 * PLAIN, GROUPS))
CTURNS = GPAIRS - PLAIN
HP = P // K
NORM_BEHIND = (8, 20, 24)
OH_FIRST = 4 * CT
W_FIRST = 12
STEPS = BT // 2
IQ = 8
ROW = -(-TG // 4) * 4
SPR = TG + 1


def build(nc, x, src, dst, U, Dmat, head_w, out):
    f32, i32 = mybir.dt.float32, mybir.dt.int32
    ALU, ACT, AX = mybir.AluOpType, mybir.ActivationFunctionType, mybir.AxisListType
    ctx = ExitStack()
    with ctx:
        def sb(name, shape, dt=f32):
            return ctx.enter_context(nc.sbuf_tensor(name, shape, dt))

        def sem(name):
            return ctx.enter_context(nc.semaphore(name))

        def sem4(name):
            return [sem(f"{name}{p}") for p in range(SLOTS)]

        def sem2(name):
            return [sem(f"{name}{p}") for p in range(2)]

        ps = [ctx.enter_context(nc.psum_tensor(f"bank{b}", [P, 512], f32)) for b in range(8)]

        z_dram = nc.dram_tensor("z_dram", [N + WIN, F], f32).ap()
        num_dram = nc.dram_tensor("num_dram", [F, N + GE], f32).ap()
        den_dram = nc.dram_tensor("den_dram", [K, N + GE], f32).ap()
        rden_dram = nc.dram_tensor("rden_dram", [K, N], f32).ap()
        dst_pad = nc.dram_tensor("dst_pad", [1, E + 2], i32).ap()

        ident = sb("ident", [P, P])
        iota_i = sb("iota_i", [P, P + 1], i32)
        iota_row = sb("iota_row", [P, P])
        iota_col = sb("iota_col", [P, 1])
        ones = sb("ones", [1, P])
        minus1 = sb("minus1", [1, 1], i32)
        U_sb = sb("U_sb", [P, HALVES, F])
        Mh = sb("Mh", [P, HALVES, D])
        G2 = sb("G2", [P, D])
        hw = sb("hw", [P, K])
        hwm = sb("hwm", [P, 1])
        hws = sb("hws", [P, 1])
        src_col = sb("src_col", [ET, TILES], i32)
        node_col = sb("node_col", [P, TILES])
        dst_rel = sb("dst_rel", [ET, TILES])
        first_i = sb("first_i", [1, GROUPS, ROW], i32)
        off_i = sb("off_i", [1, GROUPS, ROW], i32)
        gap_i = sb("gap_i", [1, GROUPS], i32)
        xs = [sb(f"xs{s}", [P, 2, HT, D]) for s in range(XB)]
        xT = [sb(f"xT{m}", [P, 2, HALVES, P]) for m in range(STEPS)]
        zo = [sb(f"zo{s}", [P, 2, HT, F]) for s in range(SLOTS)]
        idx_g = [sb(f"idx_g{p}", [ET, TG], i32) for p in range(2)]
        zs = [sb(f"zs{p}", [ET, TG, F]) for p in range(2)]
        zw = [sb(f"zw{p}", [WIN, TG, F]) for p in range(2)]
        dst_b = sb("dst_b", [P, TG, ET], i32)
        rows_i = [sb(f"rows_i{p}", [KJ, ET + 2], i32) for p in range(2)]
        nodes_g = sb("nodes_g", [P, TG])
        rel_g = sb("rel_g", [ET, TG])
        spread = [sb(f"spread{p}", [WIN, CT, ET]) for p in range(2)]
        onehot = sb("onehot", [P, TG, WIN])
        prod = sb("prod", [ET, CT, K, R])
        logit = sb("logit", [ET, K, TG])
        rows = sb("rows", [KJ, ET + 2])
        pen = sb("pen", [KJ, ET + 1])
        pen_first = sb("pen_first", [KJ, ET])
        pen_last = sb("pen_last", [KJ, ET])
        fmax = sb("fmax", [KJ, ET])
        rmax = sb("rmax", [KJ, ET])
        m1 = sb("m1", [KJ, ET])
        m2 = sb("m2", [KJ, ET])
        shifted = sb("shifted", [KJ, ET])
        edge4 = sb("edge4", [1, 4, KJ])
        differ = sb("differ", [1, 2, KJ])
        fpen = sb("fpen", [1, K, SPR])
        bpen = sb("bpen", [1, K, SPR])
        fval = sb("fval", [1, K, SPR])
        bval = sb("bval", [1, K, SPR])
        run = sb("run", [1, K, SPR])
        back = sb("back", [1, K, SPR])
        besides = sb("besides", [1, 2, KJ])
        rrow = sb("rrow", [1, 2, K, R])
        rrow2 = sb("rrow2", [1, 2, K, R])
        rscale = sb("rscale", [P, 1])
        W = sb("W", [P, TG, 2, F])
        agg = [sb(f"agg{p}", [P, GE + WIN]) for p in range(2)]
        raw_i = onehot[:ET, :, :].rearrange("p t e -> p (t e)")[:, 0:2 * ET * IQ].bitcast(i32).rearrange("p (s c) -> p s c", s=2)
        raw_f = W[:ET, :, :, :].rearrange("p t a f -> p (t a f)")[:, 0:2 * ET * IQ].rearrange("p (s c) -> p s c", s=2)
        def part(buf, start, size):
            return buf[:, :, :].rearrange("p t f -> p (t f)")[:, start:start + size]
        xs.append(part(dst_b, 0, BT * D).bitcast(f32).rearrange("p (h t d) -> p h t d", h=2, t=HT))
        dst_col = part(zs[0], 0, TILES)
        first_all = part(zw[0], 0, TILES)
        D_sb = part(zw[1], 0, HALVES * D).rearrange("p (h d) -> p h d", h=HALVES)
        DtD = part(zw[1], HALVES * D, HALVES * D).rearrange("p (h d) -> p h d", h=HALVES)
        Uw = part(zw[1], 2 * HALVES * D, HALVES * 2 * F).rearrange("p (h a f) -> p h a f", h=HALVES, a=2)
        rden = [sb(f"rden{p}", [P, GB * BN // HP]) for p in range(2)]
        nd = [sb(f"nd{p}", [P, 2, HB]) for p in range(2)]
        aggn = [sb(f"aggn{p}", [P, HT, P]) for p in range(2)]
        XT_BANK = (0, 1, 4, 5)
        AB, LI = P, P + 2 * KJ
        stats = sb("stats", [P, BT, 6])
        mv = [sb(f"mv{p}", [P, BT, 2]) for p in range(2)]
        varm = [sb(f"varm{p}", [P, 2, BT]) for p in range(2)]
        minus_half = sb("minus_half", [P, BT])
        rstd = [sb(f"rstd{p}", [P, BT]) for p in range(2)]
        nmr = [sb(f"nmr{p}", [P, BT]) for p in range(2)]

        const_step = sem("const_step")
        w_in = sem("w_in")
        pad_out = sem("pad_out")
        idx_float = sem("idx_float")
        idx_ps = sem("idx_ps")
        idx_sb = sem("idx_sb")
        prep_pe = sem("prep_pe")
        prep_dve = sem("prep_dve")
        prep_act = sem("prep_act")
        gate = sem("gate")
        x_in = sem4("x_in")
        xt_ps = sem4("xt_ps")
        xt_sb = [sem(f"xt_sb{m}") for m in range(STEPS)]
        xt_used = [sem(f"xt_used{m}") for m in range(STEPS)]
        z_sb = sem2("z_sb")
        z_out = sem4("z_out")
        idx_ready = sem2("idx_ready")
        gathered = [[sem(f"gathered{p}_{c}") for c in range(CHUNKS)] for p in range(2)]
        zw_in = sem2("zw_in")
        rows_in = sem2("rows_in")
        cols_g = sem("cols_g")
        spread_done = sem2("spread_done")
        zd_ps = sem2("zd_ps")
        prod_done = sem2("prod_done")
        logit_done = sem2("logit_done")
        oh_done = sem("oh_done")
        flag_step = sem("flag_step")
        flag_ps = sem("flag_ps")
        lrow_ps = sem("lrow_ps")
        scan_step = sem("scan_step")
        ab_ps = sem("ab_ps")
        chain_step = sem("chain_step")
        li_ps = sem("li_ps")
        r_exp = sem("r_exp")
        r_ps = sem("r_ps")
        shifted_ps = sem("shifted_ps")
        p_done = sem("p_done")
        w_done = sem2("w_done")
        agg_ps = sem("agg_ps")
        agg_step = sem("agg_step")
        flushed = sem2("flushed")
        x2_in = [sem(f"x2_in{s}") for s in range(XB)]
        den_in = sem2("den_in")
        rden_sb = sem2("rden_sb")
        rden_out = sem2("rden_out")
        nd_in = sem2("nd_in")
        quot = sem2("quot")
        xt2_ps = sem2("xt2_ps")
        xt2_sb = [sem(f"xt2_sb{m}") for m in range(2)]
        g_ps = sem2("g_ps")
        h_done = sem2("h_done")
        stat_step = sem2("stat_step")
        norm_step = sem2("norm_step")
        normed = sem2("normed")
        out_done = [sem(f"out_done{s}") for s in range(XB)]

        CONSTS = 14
        W_IN = 16 * 9
        PREP_IDX = 9
        PREP = 21
        FLAG, SCAN, CHAIN, AGG, STAT = 9, 5, 9, 2 + 2 * TG, 2 * BT + 2

        def block_base(b):
            return LAST_BASE if isinstance(b, int) and b == NBLOCKS - 1 else b * BN

        def block_rows(t, base):
            return t[bass.ds(base, BN), :].rearrange("(h p t) d -> p h (t d)", h=2, t=HT)

        def blocks(eng, body):
            def turn(i, slots):
                for s in range(slots):
                    body(i, s, s % 2, i * SLOTS + s, i * (SLOTS // 2) + s // 2)
            turn(0, SLOTS)
            with eng.Fori(1, BTURNS) as i:
                turn(i, SLOTS)
            turn(BTURNS, NBLOCKS - BTURNS * SLOTS)

        def group_pairs(eng, body):
            for par in range(2):
                body(0, par, par, None)
            with eng.Fori(1, PLAIN) as i:
                for par in range(2):
                    body(i, par, i * 2 + par, None)
            for par in range(2):
                body(PLAIN, par, 2 * PLAIN + par, 0)
            with eng.Fori(PLAIN + 1, GPAIRS) as i:
                for par in range(2):
                    body(i, par, i * 2 + par, i - PLAIN)

        def last_halves():
            return [(b // TB, b // GB % 2, range(b % TB, b % TB + min(GB, NBLOCKS - b)))
                    for b in range(CTURNS * TB, NBLOCKS, GB)]

        def last_blocks():
            return [(ti, j) for ti, half, js in last_halves() for j in js]

        def den_range(ti, half):
            base, n = (ti * 2 + half) * GB * BN, GB * BN
            if isinstance(ti, int):
                n = min(n, N - base)
            return bass.ds(base, n), n // HP

        def block_of(ti, j):
            return ti * TB + j, j % 2, ti * (TB // 2) + j // 2, j % XB, ti * (TB // XB) + j // XB

        def free(eng, sem_, value):
            if not isinstance(value, int) or value > 0:
                eng.wait_ge(sem_, value)

        def z_stored(eng):
            for s in range(SLOTS):
                eng.wait_ge(z_out[s], 16 * len(range(s, NBLOCKS, SLOTS)))

        def row_values(eng_type, table, g, limit, first=0, end=TG):
            return nc.values_load_multi_w_load_instructions(
                table[0:1, bass.ds(g, 1), first:end].rearrange("a g t -> a (g t)"), engines=(eng_type,),
                min_val=0, max_val=limit)[1]

        def passed(eng):
            eng.sem_inc(gate, 1)

        block = ctx.enter_context(nc.Block())

        @block.sync
        def _(sp):
            for h in range(HALVES):
                sp.dma_start(U_sb[:, h, :].rearrange("p (k r) -> p k r", k=K),
                             U[:, h * P:(h + 1) * P, :].rearrange("k p r -> p k r")).then_inc(w_in, 16)
                sp.dma_start(D_sb[:, h, :], Dmat[h * P:(h + 1) * P, :]).then_inc(w_in, 16)
            sp.dma_start(hw[:, :], head_w.rearrange("(a k) -> a k", a=1).to_broadcast([P, K])).then_inc(w_in, 16)
            sp.dma_start(raw_i[:, 0, :], src.rearrange("(q c) -> q c", q=ET)).then_inc(w_in, 16)
            sp.dma_start(raw_i[:, 1, :], dst.rearrange("(q c) -> q c", q=ET)).then_inc(w_in, 16)
            sp.dma_start(dst_pad[0:1, 1:E + 1].rearrange("a (q c) -> (a q) c", q=ET),
                         dst.rearrange("(q c) -> q c", q=ET)).then_inc(pad_out, 16)
            sp.wait_ge(const_step, 3)
            sp.dma_start(dst_pad[0:1, 0:1], minus1[:, :]).then_inc(w_in, 16)
            sp.dma_start(dst_pad[0:1, E + 1:E + 2], minus1[:, :]).then_inc(w_in, 16)
            sp.wait_ge(const_step, 4)
            sp.dma_start(z_dram[N:N + WIN, :], agg[0][:, 0:F]).then_inc(pad_out, 16)

            def load_first(i, s, par, b, n):
                free(sp, xt_ps[s], 4 * i)
                sp.dma_start(xs[s][:, :, :, :].rearrange("p h t d -> p h (t d)"),
                             block_rows(x, block_base(b))).then_inc(x_in[s], 16)
                if isinstance(b, int) and b < SLOTS:
                    return
                store_z(i - 1, s, par, b - SLOTS, n - SLOTS // 2)

            def store_z(i, s, par, b, n):
                sp.wait_ge(z_sb[par], n + 1)
                if isinstance(b, int) and b == NBLOCKS - 1:
                    sp.wait_ge(z_out[(b - 1) % SLOTS], 16 * ((b - 1) // SLOTS + 1))
                sp.dma_start(z_dram[bass.ds(block_base(b), BN), :].rearrange("(h p t) f -> p h (t f)", h=2, t=HT),
                             zo[s][:, :, :, :].rearrange("p h t f -> p h (t f)")).then_inc(z_out[s], 16)
            blocks(sp, load_first)
            for b in range(NBLOCKS - SLOTS, NBLOCKS):
                store_z(b // SLOTS, b % SLOTS, b % 2, b, b // 2)

            sp.wait_ge(prep_dve, PREP_IDX)
            sp.wait_ge(pad_out, 32)
            sp.wait_ge(w_in, W_IN)
            z_stored(sp)

            def load_group(i, par, g, ti):
                if ti is not None:
                    sp.wait_ge(flushed[par], 32 * i)
                    passed(sp)
                    load_den(ti, par)
                v = dst_pad[0:1, bass.ds(g * GE, GE)].rearrange("a (t e) -> (a t) e", t=TG)
                v = bass.AP(v.tensor, v.offset, [[0, K], [ET, TG], [1, ET + 2]], runtime_checks=v.runtime_checks)
                free(sp, zd_ps[par], CHUNKS * i)
                passed(sp)
                sp.dma_start(rows_i[par][:, :], v).then_inc(rows_in[par], 16)
                for t, n0 in enumerate(row_values(mybir.EngineType.SP, first_i, g, N - 1)):
                    sp.dma_start(zw[par][:, t, :], z_dram[bass.ds(n0, WIN), :]).then_inc(zw_in[par], 16)
                free(sp, spread_done[1 - par], CHUNKS * (i + par))
                passed(sp)
                sp.dma_start(dst_b[:, :, :].rearrange("p t e -> p (t e)"),
                             dst_pad[0:1, bass.ds(g * GE + 1, GE)].to_broadcast([P, GE])).then_inc(rows_in[par], 16)
                if ti is not None:
                    load_x(ti, GB * par)
                    store_rden(ti, par)
                    for j in range(GB * par, GB * (par + 1)):
                        load_sums(ti, j)
                        if j > GB * par:
                            load_x(ti, j)

            def load_den(ti, par):
                cols, w = den_range(ti, par)
                free(sp, rden_out[par], 16 * ti)
                passed(sp)
                sp.dma_start(rden[par][:, 0:w], den_dram[:, cols].rearrange("k (c n) -> k c n", c=HP)
                             ).then_inc(den_in[par], 16)

            def store_rden(ti, par):
                cols, w = den_range(ti, par)
                sp.wait_ge(rden_sb[par], 2 * (ti + 1))
                passed(sp)
                sp.dma_start(rden_dram[:, cols].rearrange("k (c n) -> k c n", c=HP), rden[par][:, 0:w]
                             ).then_inc(rden_out[par], 16)

            def load_sums(ti, j):
                b, par, n, s, ns = block_of(ti, j)
                base = block_base(b)
                free(sp, quot[par], n)
                passed(sp)
                sp.wait_ge(rden_out[j // GB], 16 * (ti + 1))
                passed(sp)
                for h in range(2):
                    cols = bass.ds(base + h * HB, HB)
                    sp.dma_start(nd[par][h * F:(h + 1) * F, 0, :], num_dram[:, cols]).then_inc(nd_in[par], 16)
                    sp.dma_start(nd[par][h * F:(h + 1) * F, 1, :],
                                 rden_dram[:, cols].unsqueeze(1).to_broadcast([K, R, HB])).then_inc(nd_in[par], 16)

            def load_x(ti, j):
                b, par, n, s, ns = block_of(ti, j)
                free(sp, out_done[s], 16 * ns)
                passed(sp)
                sp.dma_start(xs[s][:, :, :, :].rearrange("p h t d -> p h (t d)"),
                             block_rows(x, block_base(b))).then_inc(x2_in[s], 16)

            group_pairs(sp, load_group)
            for n in range(2):
                halves = last_halves()[0:1] if n == 0 else last_halves()[1:]
                sp.wait_ge(flushed[n], 32 * GPAIRS)
                for ti, half, js in halves:
                    load_den(ti, half)
                for ti, half, js in halves:
                    store_rden(ti, half)
                for ti, half, js in halves:
                    for j in js:
                        load_x(ti, j)
                        load_sums(ti, j)
            for s in range(XB):
                sp.wait_ge(out_done[s], 16 * len(range(s, NBLOCKS, XB)))

        @block.gpsimd
        def _(pool):
            pool.memset(ident[:, :], 0.0).then_inc(const_step, 1)
            pool.memset(ones[:, :], 1.0).then_inc(const_step, 1)
            pool.memset(minus1[:, :], -1).then_inc(const_step, 1)
            pool.memset(agg[0][:, :], 0.0).then_inc(const_step, 1)
            pool.memset(agg[1][:, :], 0.0).then_inc(const_step, 1)
            pool.iota(iota_i[:, 0:P], [[1, P]], base=0, channel_multiplier=0).then_inc(const_step, 1)
            pool.iota(iota_i[:, P:P + 1], [[0, 1]], base=0, channel_multiplier=1).then_inc(const_step, 1)
            pool.wait_ge(const_step, 7)
            pool.affine_select(out=ident[:, :], in_=ident[:, :], compare_op=ALU.not_equal, fill=1.0,
                               base=0, pattern=[[-1, P]], channel_multiplier=1).then_inc(const_step, 1)
            pool.memset(fpen[:, :, 0:1], -BIG).then_inc(const_step, 1)
            pool.memset(bpen[:, :, TG:SPR], -BIG).then_inc(const_step, 1)
            pool.memset(bval[:, :, TG:SPR], -BIG).then_inc(const_step, 1)
            pool.memset(run[:, :, :], -BIG).then_inc(const_step, 1)
            pool.memset(gap_i[:, 0:1], 0).then_inc(const_step, 1)
            pool.memset(minus_half[:, :], -0.5).then_inc(const_step, 1)

            pool.wait_ge(prep_dve, PREP_IDX)
            z_stored(pool)

            def gather(i, par, g, ti):
                for c in range(CHUNKS):
                    free(pool, gathered[par][c], i * CT * 16)
                pool.tensor_copy(idx_g[par][:, :], src_col[:, bass.ds(g * TG, TG)]).then_inc(idx_ready[par], 1)
                free(pool, w_done[par], 2 * i)
                pool.wait_ge(idx_ready[par], i + 1)
                passed(pool)
                for t in range(TG):
                    pool.indirect_dma_start(
                        out=zs[par][:, t, :], out_offset=None, in_=z_dram[:, :],
                        in_offset=bass.IndirectOffsetOnAxis(ap=idx_g[par][:, t:t + 1], axis=0),
                        ).then_inc(gathered[par][t // CT], 16)
                    if t in NORM_BEHIND and ti is not None:
                        k = NORM_BEHIND.index(t)
                        if par == 1:
                            normalise(ti, k)
                        elif not isinstance(ti, int):
                            normalise(ti - 1, GB + k)

            def normalise(ti, j):
                b, par, n, s, ns = block_of(ti, j)
                pool.wait_ge(stat_step[par], STAT * (n + 1))
                free(pool, normed[par], BT * n)
                pool.tensor_tensor(rstd[par][:, :], varm[par][:, 0, :], minus_half[:, :], ALU.pow
                                   ).then_inc(norm_step[par], 1)
                pool.wait_ge(norm_step[par], 2 * n + 1)
                pool.tensor_tensor(nmr[par][:, :], varm[par][:, 1, :], rstd[par][:, :], ALU.mult
                                   ).then_inc(norm_step[par], 1)
                pool.wait_ge(norm_step[par], 2 * n + 2)
                passed(pool)
                for t in range(BT):
                    v = xs[s][:, t // HT, t % HT, :]
                    pool.tensor_scalar(v, v, rstd[par][:, t:t + 1], nmr[par][:, t:t + 1], ALU.mult, ALU.add
                                       ).then_inc(normed[par], 1)
                pool.wait_ge(normed[par], BT * (n + 1))
                if isinstance(b, int) and b == NBLOCKS - 1:
                    pool.wait_ge(out_done[(b - 1) % XB], 16 * ((b - 1) // XB + 1))
                pool.dma_start(block_rows(out, block_base(b)),
                               xs[s][:, :, :, :].rearrange("p h t d -> p h (t d)")).then_inc(out_done[s], 16)
            group_pairs(pool, gather)
            for j in range(GB):
                normalise(CTURNS - 1, GB + j)
            for ti, j in last_blocks():
                normalise(ti, j)

        @block.tensor
        def _(pe):
            pe.wait_ge(const_step, CONSTS)
            n = 0
            for s in range(2):
                for c in range(IQ):
                    pe.wait_ge(idx_float, 2)
                    if n >= 2:
                        pe.wait_ge(idx_sb, n - 1)
                    pe.transpose(ps[n % 2][:ET, 0:ET], raw_f[:, s, c * ET:(c + 1) * ET],
                                 ident[:ET, :ET]).then_inc(idx_ps, 1)
                    n += 1
            pe.wait_ge(idx_sb, 2 * IQ)
            for c in range(2):
                pe.matmul(ps[2 + c][:, 0:TILES // 2], ones[:, :], dst_col[0:1, c * TILES // 2:(c + 1) * TILES // 2],
                          start=True, stop=True).then_inc(prep_pe, 1)
            pe.wait_ge(w_in, W_IN)
            for a in range(HALVES):
                for b in range(HALVES):
                    mm = pe.matmul(ps[4 + a][:, 0:D], D_sb[:, b, a * P:(a + 1) * P], D_sb[:, b, :],
                                   start=b == 0, stop=b == HALVES - 1)
                mm.then_inc(prep_pe, 1)
            pe.wait_ge(prep_act, 3)
            for a in range(HALVES):
                for b in range(HALVES):
                    mm = pe.matmul(ps[6 + a][:, 0:D], DtD[:, b, a * P:(a + 1) * P], D_sb[:, b, :],
                                   start=b == 0, stop=b == HALVES - 1)
                mm.then_inc(prep_pe, 1)
            pe.wait_ge(prep_dve, PREP)
            for h in range(HALVES):
                mm = pe.matmul(ps[4][:, 0:D], Uw[:, h, :, :].rearrange("p a f -> p (a f)"), Mh[:, h, :],
                               start=h == 0, stop=h == HALVES - 1)
            mm.then_inc(prep_pe, 1)

            def transposes(m, x_sb, bank, ps_sem):
                for u in range(2):
                    t = 2 * m + u
                    for h in range(HALVES):
                        tr = pe.transpose(ps[bank][:, (u * HALVES + h) * P:(u * HALVES + h + 1) * P],
                                          x_sb[:, t // HT, t % HT, h * P:(h + 1) * P], ident[:, :])
                tr.then_inc(ps_sem, 1)

            pe.wait_ge(prep_act, 4)

            def block_a(i, s, par, b, n):
                pe.wait_ge(x_in[s], 16 * (i + 1))

                def zmm(m):
                    pe.wait_ge(xt_sb[m], b + 1)
                    if m == 0:
                        free(pe, z_sb[par], n)
                    for u in range(2):
                        t = 2 * m + u
                        for h in range(HALVES):
                            mm = pe.matmul(ps[2 + par][:, t * F:(t + 1) * F], xT[m][:, u, h, :], U_sb[:, h, :],
                                           start=h == 0, stop=h == HALVES - 1)
                    mm.then_inc(xt_used[m], 1)
                for m in range(STEPS):
                    free(pe, xt_sb[m], b)
                    transposes(m, xs[s], XT_BANK[m], xt_ps[s])
                    if m >= 2:
                        zmm(m - 2)
                zmm(STEPS - 2)
                zmm(STEPS - 1)
            blocks(pe, block_a)

            def block_step(ti, j, m):
                b, par, n, s, ns = block_of(ti, j)
                if m == 0:
                    pe.wait_ge(x2_in[s], 16 * (ns + 1))
                if m < STEPS:
                    free(pe, xt2_sb[m % 2], 2 * b + m // 2)
                    transposes(m, xs[s], 4 + m % 2, xt2_ps[par])
                if m:
                    gradient(ti, j, m - 1)

            def gradient(ti, j, m):
                b, par, n, s, ns = block_of(ti, j)
                pe.wait_ge(xt2_sb[m % 2], 2 * b + m // 2 + 1)
                if m == 0:
                    pe.wait_ge(quot[par], n + 1)
                if m >= 2:
                    pe.wait_ge(h_done[par], 4 * n + m - 1)
                else:
                    free(pe, h_done[1 - par], 4 * (n + par) + m - 1)
                for u in range(2):
                    t = 2 * m + u
                    hf, uu = t // HT, t % HT
                    o = ps[6 + m % 2][:, u * D:(u + 1) * D]
                    for h in range(HALVES):
                        pe.matmul(o, xT[m % 2][:, u, h, :], Mh[:, h, :], start=h == 0, stop=False)
                    mm = pe.matmul(o, aggn[par][hf * F:(hf + 1) * F, uu, :], G2[hf * F:(hf + 1) * F, :],
                                   start=False, stop=True)
                mm.then_inc(g_ps[par], 1)

            def group_b(i, par, g, ti):
                def beside(*steps):
                    if ti is not None:
                        for k in steps:
                            block_step(ti, GB * par + k // (STEPS + 1), k % (STEPS + 1))

                beside(0, 1)
                pe.wait_ge(flag_step, FLAG * g + 1)
                free(pe, agg_step, (g - 1) * AGG + 1)
                for n, c in enumerate((0, 1, ET, ET + 1)):
                    tr = pe.transpose(ps[3][0:1, n * KJ:(n + 1) * KJ], rows[:, c:c + 1], ident[:KJ, :KJ])
                tr.then_inc(flag_ps, 1)
                pe.wait_ge(zw_in[par], (i + 1) * TG * 16)
                for c in range(CHUNKS):
                    pe.wait_ge(spread_done[par], i * CHUNKS + c + 1)
                    if c:
                        pe.wait_ge(prod_done[par], i * CHUNKS + c)
                    else:
                        free(pe, prod_done[1 - par], (i + par) * CHUNKS)
                    for u in range(CT):
                        mm = pe.matmul(ps[2][:ET, u * F:(u + 1) * F], spread[c % 2][:, u, :],
                                       zw[par][:, c * CT + u, :], start=True, stop=True)
                    mm.then_inc(zd_ps[par], 1)
                    beside(c + 2)
                pe.wait_ge(logit_done[par], (i + 1) * CHUNKS)
                pe.wait_ge(flag_step, FLAG * g + 6)
                pe.transpose(ps[3][:KJ, 0:ET], logit[:, :, :].rearrange("p k t -> p (k t)"),
                             ident[:ET, :ET]).then_inc(lrow_ps, 1)
                beside(7)
                pe.wait_ge(scan_step, SCAN * g + 2)
                pe.transpose(ps[3][0:1, AB:AB + KJ], rmax[:, 0:1], ident[:KJ, :KJ])
                pe.transpose(ps[3][0:1, AB + KJ:AB + 2 * KJ], rmax[:, ET - 1:ET], ident[:KJ, :KJ]).then_inc(ab_ps, 1)
                beside(8)
                pe.wait_ge(chain_step, CHAIN * g + 7)
                pe.matmul(ps[3][:KJ, LI:LI + 1], besides[:, 0, :], ones[:, 0:1], start=True, stop=True)
                pe.matmul(ps[3][:KJ, LI + 1:LI + 2], besides[:, 1, :], ones[:, 0:1], start=True, stop=True).then_inc(li_ps, 1)
                beside(9)
                pe.wait_ge(scan_step, SCAN * g + 5)
                passed(pe)
                pe.wait_ge(r_exp, g + 1)
                pe.matmul(ps[3][:, LI + 2:LI + 3], rrow2[0:1, :, :, :].rearrange("a b k r -> a (b k r)"), ones[:, 0:1],
                          start=True, stop=True).then_inc(r_ps, 1)
                pe.transpose(ps[3][:ET, AB:AB + KJ], shifted[:, :], ident[:KJ, :KJ]).then_inc(shifted_ps, 1)
                beside(10, 11)
                pe.wait_ge(w_done[par], 2 * i + 1)
                passed(pe)
                pe.wait_ge(oh_done, 2 * g + 1)
                for t in range(TG):
                    q = t // 4
                    if t == W_FIRST:
                        pe.wait_ge(w_done[par], 2 * i + 2)
                        passed(pe)
                    if t == OH_FIRST:
                        pe.wait_ge(oh_done, 2 * g + 2)
                        passed(pe)
                    if t % 4 == 0:
                        if q in (2, 4, 6):
                            beside(11 + q // 2)
                        free(pe, agg_step, g * AGG + (2 + 8 * (q - 1) if q >= 2 else 0))
                    pe.matmul(ps[q % 2][:, (t % 4) * P:(t % 4 + 1) * P], W[:ET, t, :, :].rearrange("p a f -> p (a f)"),
                              onehot[:ET, t, :], start=True, stop=True).then_inc(agg_ps, 1)
            group_pairs(pe, group_b)
            for ti, j in last_blocks():
                for m in range(STEPS + 1):
                    block_step(ti, j, m)

        @block.scalar
        def _(act):
            act.wait_ge(prep_dve, PREP_IDX + 2)
            act.activation(hw[:, :], hw[:, :], ACT.Exp, bias=hwm[:, :], accum_out=hws[:, :]).then_inc(prep_act, 1)
            for a in range(HALVES):
                act.wait_ge(prep_pe, 3 + a)
                act.activation(DtD[:, a, :], ps[4 + a][:, 0:D], ACT.Copy).then_inc(prep_act, 1)
            act.wait_ge(prep_pe, 7)
            act.activation(G2[:, :], ps[4][:, 0:D], ACT.Copy).then_inc(prep_act, 1)

            def block_a(i, s, par, b, n):
                if par == 0 and not (isinstance(b, int) and b == 0):
                    copy_z(b - 1, (s - 1) % SLOTS, i - (s == 0))
                for m in range(1, STEPS, 2):
                    act.wait_ge(xt_ps[s], 4 * i + m + 1)
                    free(act, xt_used[m], b)
                    act.activation(xT[m][:, :, :, :].rearrange("p u h n -> p (u h n)"), ps[XT_BANK[m]][:, :], ACT.Copy
                                   ).then_inc(xt_sb[m], 1)

            def copy_z(b, s, i):
                act.wait_ge(xt_used[STEPS - 1], b + 1)
                free(act, z_out[s], 16 * i)
                act.activation(zo[s][:, :, :, :].rearrange("p h t f -> p (h t f)"), ps[3][:, :], ACT.Copy
                               ).then_inc(z_sb[1], 1)
            blocks(act, block_a)
            copy_z(NBLOCKS - 1, (NBLOCKS - 1) % SLOTS, (NBLOCKS - 1) // SLOTS)

            def copy_step(ti, j, m):
                b, par, n, s, ns = block_of(ti, j)
                act.wait_ge(xt2_ps[par], 4 * n + m + 1)
                if m >= 2:
                    act.wait_ge(g_ps[par], 4 * n + m - 1)
                else:
                    free(act, g_ps[1 - par], 4 * (n + par) + m - 1)
                act.activation(xT[m % 2][:, :, :, :].rearrange("p u h n -> p (u h n)"), ps[4 + m % 2][:, :], ACT.Copy
                               ).then_inc(xt2_sb[m % 2], 1)

            def flush(i, par, g):
                n0 = act.value_load(first_i[0:1, bass.ds(g - 1, 1), 0:1].rearrange("a g t -> a (g t)"),
                                    min_val=0, max_val=N - 1)
                act.wait_ge(agg_step, g * AGG)
                passed(act)
                free(act, flushed[par], 32 * i)
                act.dma_start(num_dram[:, bass.ds(n0, GE)], agg[1 - par][0:F, 0:GE]).then_inc(flushed[1 - par], 16)
                act.dma_start(den_dram[:, bass.ds(n0, GE)], agg[1 - par][F:2 * F:R, 0:GE]).then_inc(flushed[1 - par], 16)

            def group_b(i, par, g, ti):
                def beside(*steps):
                    if ti is not None:
                        for k in steps:
                            copy_step(ti, GB * par + k // STEPS, k % STEPS)

                offs = []
                for k in range(8):
                    beside(k)
                    if k == 1 and not (isinstance(g, int) and g == 0):
                        flush(i, par, g)
                    if k >= 3 and len(offs) < TG:
                        offs += row_values(mybir.EngineType.Activation, off_i, g, GE - 1, len(offs),
                                           min(len(offs) + 8, TG))
                gap = act.value_load(gap_i[0:1, bass.ds(g, 1)], min_val=0, max_val=GE)
                act.wait_ge(chain_step, CHAIN * g + 9)
                free(act, r_ps, g)
                act.activation(rrow2[:, :, :, :].rearrange("a b k r -> a (b k r)"),
                               rrow[:, :, :, :].rearrange("a b k r -> a (b k r)"), ACT.Exp).then_inc(r_exp, 1)
                beside(8)
                act.wait_ge(shifted_ps, g + 1)
                free(act, agg_ps, g * TG)
                act.activation(W[:ET, :, 1, :].rearrange("p t (k r) -> p t k r", k=K),
                               ps[3][:ET, AB:AB + KJ].rearrange("p (k t) -> p t k", k=K).unsqueeze(3).to_broadcast([ET, TG, K, R]),
                               ACT.Exp).then_inc(p_done, 1)
                beside(9)
                act.wait_ge(r_ps, g + 1)
                free(act, agg_step, g * AGG)
                act.activation(rscale[:, :], ps[3][:, LI + 2:LI + 3], ACT.Copy).then_inc(agg_step, 1)
                act.wait_ge(agg_step, g * AGG + 1)
                free(act, flushed[par], 32 * i)
                act.activation(agg[par][:, 0:1], agg[1 - par][:, bass.ds(gap, 1)], ACT.Copy, scale=rscale[:, :]
                               ).then_inc(agg_step, 1)
                for t in range(TG):
                    bank = ps[(t // 4) % 2]
                    off = offs[t]
                    if t % 4 == 0:
                        act.wait_ge(agg_ps, g * TG + min(t + 4, TG))
                    act.wait_ge(agg_step, g * AGG + 2 + 2 * t)
                    col = agg[par][:, bass.ds(off, 1)]
                    act.activation(col, bank[:, (t % 4) * P:(t % 4) * P + 1], ACT.Identity, bias=col
                                   ).then_inc(agg_step, 1)
                    act.activation(agg[par][:, bass.ds(off + 1, WIN - 1)], bank[:, (t % 4) * P + 1:(t % 4 + 1) * P],
                                   ACT.Copy).then_inc(agg_step, 1)
            group_pairs(act, group_b)
            flush(GPAIRS, 0, GROUPS)

            for ti, j in last_blocks():
                for m in range(STEPS):
                    copy_step(ti, j, m)

        @block.vector
        def _(dve):
            dve.wait_ge(const_step, CONSTS)
            dve.tensor_copy(iota_row[:, :], iota_i[:, 0:P]).then_inc(prep_dve, 1)
            dve.tensor_copy(iota_col[:, :], iota_i[:, P:P + 1]).then_inc(prep_dve, 1)
            dve.wait_ge(w_in, W_IN)
            dve.tensor_copy(raw_f[:, 0, :], raw_i[:, 0, :]).then_inc(idx_float, 1)
            dve.tensor_copy(raw_f[:, 1, :], raw_i[:, 1, :]).then_inc(idx_float, 1)
            n = 0
            for col in (src_col, dst_col):
                for c in range(IQ):
                    dve.wait_ge(idx_ps, n + 1)
                    dve.tensor_copy(col[:, :].rearrange("p (q j) -> p j q", j=IQ)[:, c, :], ps[n % 2][:ET, 0:ET]
                                    ).then_inc(idx_sb, 1)
                    n += 1
            for c in range(2):
                half = slice(c * TILES // 2, (c + 1) * TILES // 2)
                dve.wait_ge(prep_pe, 1 + c)
                dve.tensor_copy(first_all[:, half], ps[2 + c][:, 0:TILES // 2]).then_inc(prep_dve, 1)
            dve.wait_ge(prep_dve, 4)
            dve.tensor_scalar(node_col[:, :], first_all[:, :], iota_col[:, :], None, ALU.add).then_inc(prep_dve, 1)
            dve.tensor_tensor(dst_rel[:, :], dst_col[:, :], first_all[:ET, :], ALU.subtract).then_inc(prep_dve, 1)
            by_group = first_all[0:1, :].rearrange("a (g t) -> a g t", t=TG)
            dve.tensor_copy(first_i[:, :, 0:TG], by_group).then_inc(prep_dve, 1)
            dve.tensor_tensor(off_i[:, :, 0:TG], by_group,
                              by_group[:, :, 0:1].to_broadcast([1, GROUPS, TG]), ALU.subtract).then_inc(prep_dve, 1)
            dve.tensor_tensor(gap_i[:, 1:GROUPS], by_group[:, 1:GROUPS, 0], by_group[:, 0:GROUPS - 1, 0],
                              ALU.subtract).then_inc(prep_dve, 1)

            dve.tensor_reduce(hwm[:, :], hw[:, :], AX.X, ALU.max).then_inc(prep_dve, 1)
            dve.wait_ge(prep_dve, PREP_IDX + 1)
            dve.tensor_scalar(hwm[:, :], hwm[:, :], -1.0, None, ALU.mult).then_inc(prep_dve, 1)
            dve.wait_ge(prep_act, 1)
            dve.reciprocal(hws[:, :], hws[:, :]).then_inc(prep_dve, 1)
            dve.wait_ge(prep_dve, PREP_IDX + 3)
            dve.tensor_scalar(hw[:, :], hw[:, :], hws[:, :], None, ALU.mult).then_inc(prep_dve, 1)
            dve.wait_ge(prep_dve, PREP_IDX + 4)
            for a in range(2):
                dve.tensor_tensor(Uw[:, :, a, :].rearrange("p h (k r) -> p h k r", k=K),
                                  U_sb[:, :, :].rearrange("p h (k r) -> p h k r", k=K),
                                  hw[:, :].unsqueeze(1).unsqueeze(3).to_broadcast([P, HALVES, K, R]), ALU.mult
                                  ).then_inc(prep_dve, 1)
            for a in range(HALVES):
                dve.wait_ge(prep_pe, 5 + a)
                dve.tensor_tensor(Mh[:, a, :], D_sb[:, a, :], ps[6 + a][:, 0:D], ALU.subtract).then_inc(prep_dve, 1)
            dve.wait_ge(prep_dve, PREP_IDX + 8)
            for a in range(HALVES):
                dve.tensor_scalar(Mh[:, a, :], Mh[:, a, :], C * ETA, None, ALU.mult).then_inc(prep_dve, 1)
            dve.wait_ge(prep_dve, PREP_IDX + 10)
            for a in range(HALVES):
                diag = Mh[:, a, a * P:(a + 1) * P]
                dve.scalar_tensor_tensor(diag, ident[:, :], C, diag, ALU.mult, ALU.add).then_inc(prep_dve, 1)

            def block_a(i, s, par, b, n):
                for m in range(0, STEPS, 2):
                    dve.wait_ge(xt_ps[s], 4 * i + m + 1)
                    free(dve, xt_used[m], b)
                    dve.tensor_copy(xT[m][:, :, :, :].rearrange("p u h n -> p (u h n)"), ps[XT_BANK[m]][:, :]
                                    ).then_inc(xt_sb[m], 1)
                    if m == 0 and par == 1:
                        copy_z(b - 1, s - 1, i)

            def copy_z(b, s, i):
                dve.wait_ge(xt_used[STEPS - 1], b + 1)
                free(dve, z_out[s], 16 * i)
                dve.tensor_copy(zo[s][:, :, :, :].rearrange("p h t f -> p (h t f)"), ps[2][:, :]
                                ).then_inc(z_sb[0], 1)
            blocks(dve, block_a)

            def quotients(par, n):
                dve.wait_ge(nd_in[par], 16 * 2 * 2 * (n + 1))
                free(dve, g_ps[par], 4 * n)
                dve.tensor_tensor(aggn[par][:, :, :], nd[par][:, 0, :].rearrange("q (n t) -> q t n", t=HT),
                                  nd[par][:, 1, :].rearrange("q (n t) -> q t n", t=HT), ALU.mult).then_inc(quot[par], 1)

            def reciprocals(ti, half):
                dve.wait_ge(den_in[half], 16 * (ti + 1))
                w = den_range(ti, half)[1]
                dve.tensor_scalar(rden[half][:, 0:w], rden[half][:, 0:w], EPS_SUM, None, ALU.add).then_inc(rden_sb[half], 1)
                dve.wait_ge(rden_sb[half], 2 * ti + 1)
                dve.reciprocal(rden[half][:, 0:w], rden[half][:, 0:w]).then_inc(rden_sb[half], 1)

            def residual_step(ti, j, m):
                b, par, n, s, ns = block_of(ti, j)
                if m == 0:
                    free(dve, stat_step[1 - par], STAT * (n + par))
                h, u = 2 * m // HT, 2 * m % HT
                dve.wait_ge(g_ps[par], 4 * n + m + 1)
                pair = xs[s][:, h, u:u + 2, :].rearrange("p t d -> p (t d)")
                dve.scalar_tensor_tensor(pair, ps[6 + m % 2][:, :], ETA * LAM, pair, ALU.max, ALU.add
                                         ).then_inc(h_done[par], 1)
                dve.wait_ge(h_done[par], 4 * n + m + 1)
                for t in (2 * m, 2 * m + 1):
                    dve.bn_stats(stats[:, t, :], xs[s][:, t // HT, t % HT, :]).then_inc(stat_step[par], 1)
                if m == (1 if j % GB < GB - 1 else 3) and not (isinstance(b, int) and b == NBLOCKS - 1):
                    quotients(1 - par, n + par)
                if m < STEPS - 1:
                    return
                dve.wait_ge(stat_step[par], STAT * n + BT)
                passed(dve)
                for t in range(BT):
                    dve.bn_aggr(mv[par][:, t, :], stats[:, t, :]).then_inc(stat_step[par], 1)
                dve.wait_ge(stat_step[par], STAT * n + 2 * BT)
                free(dve, norm_step[par], 2 * n)
                dve.tensor_scalar(varm[par][:, 0, :], mv[par][:, :, 1], EPS_LN, None, ALU.add).then_inc(stat_step[par], 1)
                dve.tensor_scalar(varm[par][:, 1, :], mv[par][:, :, 0], -1.0, None, ALU.mult).then_inc(stat_step[par], 1)

            def group_b(i, par, g, ti):
                def beside(*steps):
                    if ti is not None:
                        for k in steps:
                            residual_step(ti, GB * par + k // STEPS, k % STEPS)

                def copy_beside(k):
                    if ti is not None:
                        m = k % STEPS
                        b, blk_par, n, s, ns = block_of(ti, GB * par + k // STEPS)
                        dve.wait_ge(xt2_ps[blk_par], 4 * n + m + 1)
                        dve.wait_ge(g_ps[blk_par], 4 * n + m - 1)
                        dve.tensor_copy(xT[m % 2][:, :, :, :].rearrange("p u h n -> p (u h n)"), ps[4 + m % 2][:, :]
                                        ).then_inc(xt2_sb[m % 2], 1)

                if isinstance(ti, int) and par == 0:
                    reciprocals(0, 0)
                    quotients(0, 0)
                flag, scan, chain = FLAG * g, SCAN * g, CHAIN * g
                free(dve, spread_done[1 - par], (i + par) * CHUNKS)
                free(dve, oh_done, 2 * g)
                free(dve, flag_step, flag)
                free(dve, scan_step, scan)
                free(dve, chain_step, chain)
                dve.tensor_copy(nodes_g[:, :], node_col[:, bass.ds(g * TG, TG)]).then_inc(cols_g, 1)
                dve.tensor_copy(rel_g[:, :], dst_rel[:, bass.ds(g * TG, TG)]).then_inc(cols_g, 1)
                dve.wait_ge(rows_in[par], 16 * 2 * (i + 1))
                free(dve, flag_ps, g)
                dve.tensor_copy(rows[:, :], rows_i[par][:, :]).then_inc(flag_step, 1)
                dve.wait_ge(flag_step, flag + 1)
                dve.tensor_tensor(pen[:, :], rows[:, 1:ET + 2], rows[:, 0:ET + 1], ALU.not_equal).then_inc(flag_step, 1)
                dve.tensor_scalar(pen_first[:, :], rows[:, 1:ET + 1], rows[:, 0:1], -BIG, ALU.not_equal, ALU.mult
                                  ).then_inc(flag_step, 1)
                dve.tensor_scalar(pen_last[:, :], rows[:, 1:ET + 1], rows[:, ET + 1:ET + 2], -BIG,
                                  ALU.not_equal, ALU.mult).then_inc(flag_step, 1)
                dve.wait_ge(flag_step, flag + 2)
                dve.tensor_scalar(pen[:, :], pen[:, :], -BIG, None, ALU.mult).then_inc(flag_step, 1)

                def spreads(c):
                    if c == 0:
                        dve.wait_ge(cols_g, 2 * (g + 1))
                    if c >= 2:
                        dve.wait_ge(zd_ps[par], i * CHUNKS + c - 1)
                    else:
                        free(dve, zd_ps[1 - par], (i + par) * CHUNKS)
                    for u in range(CT):
                        t = c * CT + u
                        last = dve.tensor_scalar(spread[c % 2][:, u, :], dst_b[:, t, :], nodes_g[:, t:t + 1],
                                                 None, ALU.is_equal)
                    last.then_inc(spread_done[par], 1)

                def logits(c):
                    dve.wait_ge(zd_ps[par], i * CHUNKS + c + 1)
                    dve.wait_ge(gathered[par][c], 16 * CT * (i + 1))
                    if c == 0:
                        free(dve, lrow_ps, g)
                        free(dve, logit_done[1 - par], (i + par) * CHUNKS)
                    else:
                        dve.wait_ge(logit_done[par], i * CHUNKS + c)
                    dve.scalar_tensor_tensor(prod[:, :, :, :].rearrange("p t k r -> p (t k r)"),
                                             ps[2][:ET, 0:CT * F], float(R) ** -0.5,
                                             zs[par][:, c * CT:(c + 1) * CT, :].rearrange("p t f -> p (t f)"),
                                             ALU.mult, ALU.mult).then_inc(prod_done[par], 1)
                    dve.wait_ge(prod_done[par], i * CHUNKS + c + 1)
                    dve.tensor_reduce(logit[:, :, c * CT:(c + 1) * CT].rearrange("p k t -> p t k"),
                                      prod[:, :, :, :], AX.X, ALU.add).then_inc(logit_done[par], 1)

                def onehots(a, b):
                    if a == 0:
                        free(dve, agg_ps, g * TG)
                    for t in range(a, b):
                        last = dve.tensor_scalar(onehot[:ET, t, :], iota_row[:ET, :], rel_g[:, t:t + 1], None, ALU.is_equal)
                    if b in (OH_FIRST, TG):
                        last.then_inc(oh_done, 1)

                spreads(0)
                spreads(1)
                beside(0)
                for c in range(CHUNKS):
                    logits(c)
                    if c + 2 < CHUNKS:
                        spreads(c + 2)
                    if c in (0, 1, 3):
                        beside(c + 1 - c // 3)
                    if ti is None:
                        onehots(c * CT, (c + 1) * CT)
                dve.wait_ge(flag_ps, g + 1)
                dve.tensor_copy(edge4[:, :, :].rearrange("a n k -> a (n k)"), ps[3][0:1, 0:4 * KJ]).then_inc(flag_step, 1)
                dve.tensor_copy(fval[:, :, 0:1], run[:, :, TG:SPR]).then_inc(chain_step, 1)
                if ti is not None:
                    onehots(0, 5)
                beside(4)
                dve.wait_ge(flag_step, flag + 6)
                dve.tensor_tensor(differ[:, :, :], edge4[:, 0:2, :], edge4[:, 2:4, :], ALU.not_equal).then_inc(flag_step, 1)
                dve.wait_ge(lrow_ps, g + 1)
                dve.wait_ge(flag_step, flag + 7)
                dve.tensor_tensor_scan(fmax[:, :], pen[:, 0:ET], ps[3][:KJ, 0:ET], -BIG, ALU.add, ALU.max
                                       ).then_inc(scan_step, 1)
                dve.tensor_scalar(fpen[:, :, 1:SPR], differ[:, 0, :].rearrange("a (k t) -> a k t", k=K), -BIG, None,
                                  ALU.mult).then_inc(flag_step, 1)
                dve.tensor_scalar(bpen[:, :, 0:TG], differ[:, 1, :].rearrange("a (k t) -> a k t", k=K), -BIG, None,
                                  ALU.mult).then_inc(flag_step, 1)
                dve.wait_ge(scan_step, scan + 1)
                dve.tensor_tensor_scan(rmax[:, ::-1], pen[:, ET:0:-1], fmax[:, ::-1], -BIG, ALU.add, ALU.max
                                       ).then_inc(scan_step, 1)
                if ti is not None:
                    onehots(5, 10)
                dve.wait_ge(ab_ps, g + 1)
                dve.tensor_copy(bval[:, :, 0:TG], ps[3][0:1, AB:AB + KJ].rearrange("a (k t) -> a k t", k=K)).then_inc(chain_step, 1)
                dve.tensor_copy(fval[:, :, 1:SPR], ps[3][0:1, AB + KJ:AB + 2 * KJ].rearrange("a (k t) -> a k t", k=K)
                                ).then_inc(chain_step, 1)
                dve.wait_ge(chain_step, chain + 3)
                dve.wait_ge(flag_step, flag + 9)

                def flat(v):
                    return v[:, :, :].rearrange("a k s -> a (k s)")
                dve.tensor_tensor_scan(flat(run), flat(fpen), flat(fval), -BIG, ALU.add, ALU.max).then_inc(chain_step, 1)
                dve.tensor_tensor_scan(flat(back)[:, ::-1], flat(bpen)[:, ::-1], flat(bval)[:, ::-1], -BIG,
                                       ALU.add, ALU.max).then_inc(chain_step, 1)
                dve.wait_ge(chain_step, chain + 5)
                dve.tensor_copy(besides[:, 0, :].rearrange("a (k t) -> a k t", k=K), run[:, :, 0:TG]).then_inc(chain_step, 1)
                dve.tensor_copy(besides[:, 1, :].rearrange("a (k t) -> a k t", k=K), back[:, :, 1:SPR]).then_inc(chain_step, 1)
                free(dve, r_exp, g)
                dve.tensor_tensor(rrow[:, :, :, :], fval[:, :, 0:1].unsqueeze(1).to_broadcast([1, 2, K, R]),
                                  back[:, :, 0:1].unsqueeze(1).to_broadcast([1, 2, K, R]), ALU.subtract).then_inc(chain_step, 1)
                dve.wait_ge(chain_step, chain + 8)
                dve.tensor_scalar(rrow[:, :, :, :], rrow[:, :, :, :], 0.0, None, ALU.min).then_inc(chain_step, 1)
                if ti is not None:
                    reciprocals(ti + par, 1 - par)
                beside(5)
                dve.wait_ge(li_ps, g + 1)
                dve.scalar_tensor_tensor(m1[:, :], pen_first[:, :], ps[3][:KJ, LI:LI + 1], rmax[:, :], ALU.add, ALU.max
                                         ).then_inc(scan_step, 1)
                dve.wait_ge(scan_step, scan + 3)
                dve.scalar_tensor_tensor(m2[:, :], pen_last[:, :], ps[3][:KJ, LI + 1:LI + 2], m1[:, :], ALU.add, ALU.max
                                         ).then_inc(scan_step, 1)
                dve.wait_ge(scan_step, scan + 4)
                dve.tensor_tensor(shifted[:, :], ps[3][:KJ, 0:ET], m2[:, :], ALU.subtract).then_inc(scan_step, 1)
                if ti is not None:
                    onehots(10, 15)
                    beside(6)
                    onehots(15, OH_FIRST)
                dve.wait_ge(p_done, g + 1)
                for a, b in ((0, W_FIRST), (W_FIRST, TG)):
                    dve.tensor_tensor(W[:ET, a:b, 0, :], zs[par][:, a:b, :], W[:ET, a:b, 1, :], ALU.mult
                                      ).then_inc(w_done[par], 1)
                if ti is not None:
                    onehots(OH_FIRST, TG)
                beside(7, 8)
                copy_beside(10)
                beside(9)
                copy_beside(11)
                beside(10, 11)
            group_pairs(dve, group_b)
            for n, (ti, half, js) in enumerate(last_halves()):
                for j in js:
                    for m in range(STEPS):
                        residual_step(ti, j, m)
                    if (n, j) == (0, js[0]):
                        for later in last_halves()[1:]:
                            reciprocals(*later[:2])


def kernel(x, src, dst, L0_gnn_U, L0_gnn_Dmat, L0_gnn_head_w):
    import numpy as np
    import concourse.bacc as bacc
    from concourse.bass_utils import run_bass_kernel_spmd

    nc = bacc.Bacc("TRN2", target_bir_lowering=False, num_devices=1)
    named = {"x": x, "src": src, "dst": dst, "U": L0_gnn_U, "Dmat": L0_gnn_Dmat, "head_w": L0_gnn_head_w}
    arrays, args = {}, []
    for name, a in named.items():
        a = np.ascontiguousarray(a)
        arrays[f"in_{name}"] = a
        args.append(nc.dram_tensor(f"in_{name}", a.shape, mybir.dt.from_np(a.dtype), kind="ExternalInput").ap())
    args.append(nc.dram_tensor("out", (N, D), mybir.dt.float32, kind="ExternalOutput").ap())
    build(nc, *args)
    r = run_bass_kernel_spmd(nc, [arrays], core_ids=[0])
    return r.results[0]["out"]
```
